# Optimizing a Trainium2 kernel written in Bass

```python
import numpy as np
import jax
import jax.numpy as jnp

def _softmax(x, axis=-1):
    return jax.nn.softmax(x, axis=axis)

def _gelu(x):
    return jax.nn.gelu(x, approximate=True)

def _silu(x):
    return jax.nn.silu(x)

def _sigmoid(x):
    return jax.nn.sigmoid(x)

def _layernorm(x, axis=-1, eps=1e-05):
    m = jnp.mean(x, axis=axis, keepdims=True)
    v = jnp.var(x, axis=axis, keepdims=True)
    return (x - m) / jnp.sqrt(v + eps)

def _scatter_add(tgt, idx, src, axis=0):
    return tgt.at[idx].add(src)

def _segment_sum(src, seg, n):
    return jax.ops.segment_sum(src, seg, n)
kernel_name = 'mk_xattn_seq_d2_seqx_r4_e73dd4'

def setup_inputs(seed: int=0):
    np.random.seed(seed)
    _w = jnp.asarray

    def _rec_inputs():
        import jax
        import jax.numpy as jnp
        _rk = jax.random.key(seed)
        x = -0.0001548 + 1 * jax.random.normal(jax.random.fold_in(_rk, 1), (64, 128, 320), jnp.float32)
        _lenS = 128 - jax.random.randint(jax.random.fold_in(_rk, 7), (64,), 0, max(1, 128 // 4) + 1, jnp.int32)
        _lenS2 = 128 - jax.random.randint(jax.random.fold_in(_rk, 8), (64,), 0, max(1, 128 // 4) + 1, jnp.int32)
        _ctx_768P = jax.random.normal(jax.random.fold_in(_rk, 11), (64, 16, 192), jnp.float32)
        _ctx_768c = jax.random.dirichlet(jax.random.fold_in(_rk, 511), 0.3 * jnp.ones((16,), jnp.float32), (64, 128))
        _ctx_768t = jnp.einsum('bsk,bkd->bsd', _ctx_768c, _ctx_768P)
        _ctx_768t = _ctx_768t * jax.lax.rsqrt(jnp.mean(jnp.square(_ctx_768t)) + 1e-12) * 0.953939
        ctx_768 = 0.00141353 + 0.998943 * (_ctx_768t + 0.3 * jax.random.normal(jax.random.fold_in(_rk, 611), (64, 128, 192), jnp.float32))
        return (x, ctx_768)
    x, ctx_768 = _rec_inputs()

    def _L0_xattn_setup():
        import jax, jax.numpy as jnp
        import numpy as np
        HEADS = 8
        NUM_TOKENS = 4
        CROSS_ATTENTION_DIM = 192

        def _mha(q, k, v, heads=HEADS):
            B, Sq, H = q.shape
            Sk = k.shape[1]
            d = H // heads
            qh = q.reshape(B, Sq, heads, d).transpose(0, 2, 1, 3)
            kh = k.reshape(B, Sk, heads, d).transpose(0, 2, 1, 3)
            vh = v.reshape(B, Sk, heads, d).transpose(0, 2, 1, 3)
            scores = jnp.einsum('bhqd,bhkd->bhqk', qh, kh) * jnp.asarray(d, q.dtype) ** (-0.5)
            probs = jax.nn.softmax(scores, axis=-1)
            out = jnp.einsum('bhqk,bhkd->bhqd', probs, vh)
            return out.transpose(0, 2, 1, 3).reshape(B, Sq, H)
        key = jax.random.key(seed)
        ks = jax.random.split(key, 10)
        B, S, H, CAD, T = (4, 256, 320, CROSS_ATTENTION_DIM, NUM_TOKENS)
        sc = 0.02
        return {'hidden_states': jax.random.normal(ks[0], (B, S, H), jnp.float32), 'encoder_hidden_states': jax.random.normal(ks[1], (B, 77 + T, CAD), jnp.float32), 'Wq': jax.random.normal(ks[2], (H, H), jnp.float32) * sc, 'Wk': jax.random.normal(ks[3], (CAD, H), jnp.float32) * sc, 'Wv': jax.random.normal(ks[4], (CAD, H), jnp.float32) * sc, 'Wq_ca': jax.random.normal(ks[5], (T, H), jnp.float32) * sc, 'Wk_ca': jax.random.normal(ks[6], (CAD, H), jnp.float32) * sc, 'Wv_ca': jax.random.normal(ks[7], (CAD, H), jnp.float32) * sc, 'Wout': jax.random.normal(ks[8], (H, H), jnp.float32) * sc, 'b_out': jnp.zeros((H,), jnp.float32)}
    _L0_xattn_all = _L0_xattn_setup()
    _L0_xattn_in = {k: v for k, v in _L0_xattn_all.items() if k in ('Wq', 'Wk', 'Wv', 'Wq_ca', 'Wk_ca', 'Wv_ca', 'Wout', 'b_out')}
    del _L0_xattn_all

    def _L1_xattn_setup():
        import jax, jax.numpy as jnp
        import numpy as np
        D = 320
        H = 20
        DH = D // H
        CTX = 192
        FF_IN = 4 * D
        EPS = 1e-05

        def _ln(x, g, b):
            m = jnp.mean(x, axis=-1, keepdims=True)
            v = jnp.mean(jnp.square(x - m), axis=-1, keepdims=True)
            return (x - m) * jax.lax.rsqrt(v + EPS) * g + b

        def _attn(x, ctx, wq, wk, wv, wo, bo, heads):
            b, n, _ = x.shape
            j = ctx.shape[1]
            dh = wq.shape[1] // heads
            scale = dh ** (-0.5)
            q = (x @ wq).reshape(b, n, heads, dh).transpose(0, 2, 1, 3)
            k = (ctx @ wk).reshape(b, j, heads, dh).transpose(0, 2, 1, 3)
            v = (ctx @ wv).reshape(b, j, heads, dh).transpose(0, 2, 1, 3)
            sim = jnp.einsum('bhid,bhjd->bhij', q, k) * scale
            a = jax.nn.softmax(sim, axis=-1)
            out = jnp.einsum('bhij,bhjd->bhid', a, v)
            out = out.transpose(0, 2, 1, 3).reshape(b, n, heads * dh)
            return out @ wo + bo
        key = jax.random.key(seed)
        ks = jax.random.split(key, 24)
        r = lambda k, shp, s: jax.random.normal(k, shp, dtype=jnp.float32) * s
        d = {'x': r(ks[0], (8, 256, D), 1.0), 'context': r(ks[1], (8, 77, CTX), 1.0), 'heads': H, 'n1_g': jnp.ones((D,), jnp.float32), 'n1_b': jnp.zeros((D,), jnp.float32), 'q1': r(ks[2], (D, D), D ** (-0.5)), 'k1': r(ks[3], (D, D), D ** (-0.5)), 'v1': r(ks[4], (D, D), D ** (-0.5)), 'o1_w': r(ks[5], (D, D), D ** (-0.5)), 'o1_b': jnp.zeros((D,), jnp.float32), 'n2_g': jnp.ones((D,), jnp.float32), 'n2_b': jnp.zeros((D,), jnp.float32), 'q2': r(ks[6], (D, D), D ** (-0.5)), 'k2': r(ks[7], (CTX, D), CTX ** (-0.5)), 'v2': r(ks[8], (CTX, D), CTX ** (-0.5)), 'o2_w': r(ks[9], (D, D), D ** (-0.5)), 'o2_b': jnp.zeros((D,), jnp.float32), 'n3_g': jnp.ones((D,), jnp.float32), 'n3_b': jnp.zeros((D,), jnp.float32), 'ff_w1': r(ks[10], (D, 2 * FF_IN), D ** (-0.5)), 'ff_b1': jnp.zeros((2 * FF_IN,), jnp.float32), 'ff_w2': r(ks[11], (FF_IN, D), FF_IN ** (-0.5)), 'ff_b2': jnp.zeros((D,), jnp.float32)}
        return d
    _L1_xattn_all = _L1_xattn_setup()
    _L1_xattn_in = {k: v for k, v in _L1_xattn_all.items() if k in ('n1_g', 'n1_b', 'q1', 'k1', 'v1', 'o1_w', 'o1_b', 'n2_g', 'n2_b', 'q2', 'k2', 'v2', 'o2_w', 'o2_b', 'n3_g', 'n3_b', 'ff_w1', 'ff_b1', 'ff_w2', 'ff_b2')}
    del _L1_xattn_all
    return {'x': x, 'ctx_768': ctx_768, 'L0_xattn_Wq': _L0_xattn_in['Wq'], 'L0_xattn_Wk': _L0_xattn_in['Wk'], 'L0_xattn_Wv': _L0_xattn_in['Wv'], 'L0_xattn_Wq_ca': _L0_xattn_in['Wq_ca'], 'L0_xattn_Wk_ca': _L0_xattn_in['Wk_ca'], 'L0_xattn_Wv_ca': _L0_xattn_in['Wv_ca'], 'L0_xattn_Wout': _L0_xattn_in['Wout'], 'L0_xattn_b_out': _L0_xattn_in['b_out'], 'L1_xattn_n1_g': _L1_xattn_in['n1_g'], 'L1_xattn_n1_b': _L1_xattn_in['n1_b'], 'L1_xattn_q1': _L1_xattn_in['q1'], 'L1_xattn_k1': _L1_xattn_in['k1'], 'L1_xattn_v1': _L1_xattn_in['v1'], 'L1_xattn_o1_w': _L1_xattn_in['o1_w'], 'L1_xattn_o1_b': _L1_xattn_in['o1_b'], 'L1_xattn_n2_g': _L1_xattn_in['n2_g'], 'L1_xattn_n2_b': _L1_xattn_in['n2_b'], 'L1_xattn_q2': _L1_xattn_in['q2'], 'L1_xattn_k2': _L1_xattn_in['k2'], 'L1_xattn_v2': _L1_xattn_in['v2'], 'L1_xattn_o2_w': _L1_xattn_in['o2_w'], 'L1_xattn_o2_b': _L1_xattn_in['o2_b'], 'L1_xattn_n3_g': _L1_xattn_in['n3_g'], 'L1_xattn_n3_b': _L1_xattn_in['n3_b'], 'L1_xattn_ff_w1': _L1_xattn_in['ff_w1'], 'L1_xattn_ff_b1': _L1_xattn_in['ff_b1'], 'L1_xattn_ff_w2': _L1_xattn_in['ff_w2'], 'L1_xattn_ff_b2': _L1_xattn_in['ff_b2']}

def reference(x, ctx_768, L0_xattn_Wq, L0_xattn_Wk, L0_xattn_Wv, L0_xattn_Wq_ca, L0_xattn_Wk_ca, L0_xattn_Wv_ca, L0_xattn_Wout, L0_xattn_b_out, L1_xattn_n1_g, L1_xattn_n1_b, L1_xattn_q1, L1_xattn_k1, L1_xattn_v1, L1_xattn_o1_w, L1_xattn_o1_b, L1_xattn_n2_g, L1_xattn_n2_b, L1_xattn_q2, L1_xattn_k2, L1_xattn_v2, L1_xattn_o2_w, L1_xattn_o2_b, L1_xattn_n3_g, L1_xattn_n3_b, L1_xattn_ff_w1, L1_xattn_ff_b1, L1_xattn_ff_w2, L1_xattn_ff_b2):
    import jax
    import jax.numpy as jnp

    def _L0_xattn_ref(hidden_states, encoder_hidden_states, Wq, Wk, Wv, Wq_ca, Wk_ca, Wv_ca, Wout, b_out):
        import jax, jax.numpy as jnp
        import numpy as np
        HEADS = 8
        NUM_TOKENS = 4
        CROSS_ATTENTION_DIM = 192

        def _mha(q, k, v, heads=HEADS):
            B, Sq, H = q.shape
            Sk = k.shape[1]
            d = H // heads
            qh = q.reshape(B, Sq, heads, d).transpose(0, 2, 1, 3)
            kh = k.reshape(B, Sk, heads, d).transpose(0, 2, 1, 3)
            vh = v.reshape(B, Sk, heads, d).transpose(0, 2, 1, 3)
            scores = jnp.einsum('bhqd,bhkd->bhqk', qh, kh) * jnp.asarray(d, q.dtype) ** (-0.5)
            probs = jax.nn.softmax(scores, axis=-1)
            out = jnp.einsum('bhqk,bhkd->bhqd', probs, vh)
            return out.transpose(0, 2, 1, 3).reshape(B, Sq, H)
        residual = hidden_states
        unet_size = residual.shape[1]
        end_pos = encoder_hidden_states.shape[1] - NUM_TOKENS
        enc = encoder_hidden_states[:, :end_pos, :]
        ca = encoder_hidden_states[:, end_pos:, :]
        query = hidden_states @ Wq
        keyt = enc @ Wk
        valt = enc @ Wv
        hs = _mha(query, keyt, valt)
        ca_q1 = jnp.einsum('btc,th->bch', ca, Wq_ca)
        indices = np.linspace(0, CROSS_ATTENTION_DIM - 1, unet_size).astype(np.int64)
        ca_q1 = ca_q1[:, indices, :]
        ca_hs1 = _mha(ca_q1, residual, residual)
        ca_q2 = ca_hs1 @ Wq
        ca_k2 = ca @ Wk_ca
        ca_v2 = ca @ Wv_ca
        ca_hs2 = _mha(ca_q2, ca_k2, ca_v2)
        out = hs + ca_hs2
        out = out @ Wout + b_out
        out = out + residual
        return out

    def _L1_xattn_ref(x, context, heads, n1_g, n1_b, q1, k1, v1, o1_w, o1_b, n2_g, n2_b, q2, k2, v2, o2_w, o2_b, n3_g, n3_b, ff_w1, ff_b1, ff_w2, ff_b2):
        import jax, jax.numpy as jnp
        import numpy as np
        D = 320
        H = 20
        DH = D // H
        CTX = 192
        FF_IN = 4 * D
        EPS = 1e-05

        def _ln(x, g, b):
            m = jnp.mean(x, axis=-1, keepdims=True)
            v = jnp.mean(jnp.square(x - m), axis=-1, keepdims=True)
            return (x - m) * jax.lax.rsqrt(v + EPS) * g + b

        def _attn(x, ctx, wq, wk, wv, wo, bo, heads):
            b, n, _ = x.shape
            j = ctx.shape[1]
            dh = wq.shape[1] // heads
            scale = dh ** (-0.5)
            q = (x @ wq).reshape(b, n, heads, dh).transpose(0, 2, 1, 3)
            k = (ctx @ wk).reshape(b, j, heads, dh).transpose(0, 2, 1, 3)
            v = (ctx @ wv).reshape(b, j, heads, dh).transpose(0, 2, 1, 3)
            sim = jnp.einsum('bhid,bhjd->bhij', q, k) * scale
            a = jax.nn.softmax(sim, axis=-1)
            out = jnp.einsum('bhij,bhjd->bhid', a, v)
            out = out.transpose(0, 2, 1, 3).reshape(b, n, heads * dh)
            return out @ wo + bo
        h1 = _ln(x, n1_g, n1_b)
        x = _attn(h1, h1, q1, k1, v1, o1_w, o1_b, heads) + x
        h2 = _ln(x, n2_g, n2_b)
        x = _attn(h2, context, q2, k2, v2, o2_w, o2_b, heads) + x
        h3 = _ln(x, n3_g, n3_b)
        proj = h3 @ ff_w1 + ff_b1
        a, g = jnp.split(proj, 2, axis=-1)
        ff = a * jax.nn.gelu(g, approximate=False) @ ff_w2 + ff_b2
        return ff + x
    x = _L0_xattn_ref(x, ctx_768, L0_xattn_Wq, L0_xattn_Wk, L0_xattn_Wv, L0_xattn_Wq_ca, L0_xattn_Wk_ca, L0_xattn_Wv_ca, L0_xattn_Wout, L0_xattn_b_out)
    x = _L1_xattn_ref(x, ctx_768, 20, L1_xattn_n1_g, L1_xattn_n1_b, L1_xattn_q1, L1_xattn_k1, L1_xattn_v1, L1_xattn_o1_w, L1_xattn_o1_b, L1_xattn_n2_g, L1_xattn_n2_b, L1_xattn_q2, L1_xattn_k2, L1_xattn_v2, L1_xattn_o2_w, L1_xattn_o2_b, L1_xattn_n3_g, L1_xattn_n3_b, L1_xattn_ff_w1, L1_xattn_ff_b1, L1_xattn_ff_w2, L1_xattn_ff_b2)
    return x

_drawn_inputs = setup_inputs


def setup_inputs(seed=0):
    import zlib

    import numpy as np

    out = dict(_drawn_inputs(seed))
    spreads = {'L0_xattn_b_out': (0.0, 0.1),
     'L1_xattn_n1_g': (1.0, 0.2),
     'L1_xattn_n1_b': (0.0, 0.1),
     'L1_xattn_o1_b': (0.0, 0.1),
     'L1_xattn_n2_g': (1.0, 0.2),
     'L1_xattn_n2_b': (0.0, 0.352),
     'L1_xattn_o2_b': (0.0, 0.1),
     'L1_xattn_n3_g': (1.0, 0.2),
     'L1_xattn_n3_b': (0.0, 0.1),
     'L1_xattn_ff_b1': (0.0, 0.1),
     'L1_xattn_ff_b2': (0.0, 0.1)}
    factors = {'L0_xattn_Wq': 8.0, 'L0_xattn_Wk': 8.0, 'L0_xattn_Wq_ca': 34.404, 'L0_xattn_Wk_ca': 8.0}
    for name, (base, spread) in spreads.items():
        noise = np.random.default_rng([zlib.crc32(name.encode()), seed]).standard_normal(out[name].shape)
        drawn = base * np.exp(spread * noise) if base else spread * noise
        out[name] = jnp.asarray(drawn.astype(out[name].dtype))
    for name, factor in factors.items():
        out[name] = (out[name] * factor).astype(out[name].dtype)
    return out
```

```python
import concourse.bass as bass
from concourse import mybir
from contextlib import ExitStack

B, S, H, C = 64, 128, 320, 192
G = 4
STEPS = B // G
GS = G * S
T4 = 4
KEYS0 = S - T4
HEADS0, HEADS1 = 8, 20
D0, D1 = H // HEADS0, H // HEADS1
FF = 4 * H
FFT = FF // 128
EPS = 1e-5

CH0 = (120, 120, 80)
CH1 = (128, 128, 64)
CHC = (96, 96)
AT0, AT1 = (0, 120, 240), (0, 128, 256)
HC0, HC1 = (3, 3, 2), (8, 8, 4)

UNITS0 = ((0, 0, 3), (1, 0, 3), (2, 0, 2))
UNITS1 = ((0, 0, 4), (0, 4, 4), (1, 0, 4), (1, 4, 4), (2, 0, 4))
UNITS = (UNITS0, UNITS0, UNITS1, UNITS1)
ATT = len(UNITS)
UNITS_STEP = sum(G * len(u) for u in UNITS)

MATS0 = ("Wq", "Wout")
MATS1 = ("q1", "k1", "v1", "o1_w", "q2", "o2_w", "ff_w1")
MATSC = ("Wk", "Wv", "Wk_ca", "Wv_ca", "k2", "v2")


def first_jobs(stages):
    at, n = {}, 0
    for name, jobs in stages:
        at[name] = n
        n += jobs
    return at, n


A_AT, A_STEP = first_jobs((("Q0T", 3), ("Q1caT", 3), ("V0", G), ("V2", G), ("Q2caT", 3),
                           ("Q1T", 3), ("V1", G), ("Q2T", 3), ("gates", FFT)))
V_AT, V_STEP = first_jobs((("K0T", 3), ("kca", 1), ("vca", 1), ("K2T", 3), ("att0", G * 3), ("att1", G * 3),
                           ("ca_hsT", G), ("s4", 1), ("p4T", 1), ("ca_hs2", G), ("out0", 3 * G), ("K1T", 3),
                           ("att2", G * 5), ("out1", 3 * G), ("att3", G * 5), ("out2", 3 * G),
                           ("values", FFT), ("y", G)))
LINKS_STEP = ATT * G + 2 * 3 * G + 3


def unit_of(att, b, u=0):
    return sum(G * len(UNITS[a]) for a in range(att)) + b * len(UNITS[att]) + u


def build(nc, d, out):
    f32 = mybir.dt.float32
    ALU, ACT, AX = mybir.AluOpType, mybir.ActivationFunctionType, mybir.AxisListType
    ctx = ExitStack()
    with ctx:
        def sb(name, shape):
            return ctx.enter_context(nc.sbuf_tensor(name, shape, f32))

        def sem(name):
            return ctx.enter_context(nc.semaphore(name))

        w = {}
        for n in MATS0 + MATS1:
            w[n] = sb("w_" + n, [128, 3, 2 * FF if n == "ff_w1" else H])
        for n in MATSC:
            w[n] = sb("w_" + n, [96, 2, H])
        w_ff2 = sb("w_ff2", [128, FFT, H])
        w_qca = sb("w_qca", [T4, H])
        ident = sb("ident", [128, 128])
        mask0 = sb("mask0", [120, 3])
        mask1 = sb("mask1", [128, 8])
        maskv = sb("maskv", [128, H])
        bias = sb("bias", [128, 4, H])
        ln_g = sb("ln_g", [128, 3, 3])
        ln_b = sb("ln_b", [128, 3, 3])
        ff_b = sb("ff_b", [128, 2, FFT])
        eps, waited = sb("eps", [128, 1]), sb("waited", [128, 1])

        xT = sb("xT", [120, 3, GS])
        cT = sb("cT", [96, 2, GS])
        caG = sb("caG", [T4, GS])
        xin = sb("xin", [128, G, H])
        HS = xin
        xV = sb("xV", [128, G, HEADS0, D0 + 1])
        carep = sb("carep", [96, 2, G, HEADS0, T4])
        QA, QB = sb("QA", [128, 3, GS]), sb("QB", [128, 3, GS])
        KA, KB = sb("KA", [128, 3, GS]), sb("KB", [128, 3, GS])
        KM = sb("KM", [128, 2, HEADS1 * S])
        V0 = sb("V0", [128, G, HEADS0, D0 + 1])
        V1 = sb("V1", [128, G, HEADS1, D1 + 1])
        V2 = sb("V2", [128, G, HEADS1, D1 + 1])
        P = sb("P", [128, 3, 4 * S])
        PT = sb("PT", [128, 2, 4 * S])
        nmax = sb("nmax", [128, 3, 4])
        rden = sb("rden", [128, HEADS1])
        O = sb("O", [128, G, H])
        hT = sb("hT", [128, 3, GS])
        kca = sb("kca", [120, 3, G, 3, T4])
        vca = sb("vca", [128, H])
        p4 = P[:, 0, 0:G * HEADS0 * T4].rearrange("p (q t) -> p q t", t=T4)
        p4T = P[:, 1, 0:128]
        m4 = sb("m4", [128, G * HEADS0])
        X = sb("X", [128, G, H])
        XH = O
        stats = sb("stats", [128, G, 6])
        mv = sb("mv", [128, G, 2])
        sd = sb("sd", [128, G, 1])
        gate = PT
        F = KM[:, :, :].rearrange("p a n -> p (a n)").rearrange("p (t n) -> p t n", n=GS)

        banks = [ctx.enter_context(nc.psum_tensor(f"bank{i}", [128, 512], f32)) for i in range(8)]
        s_bank, o_bank, a_bank, v_bank = banks[0:3], banks[3], banks[4:6], banks[6:8]

        consts_loaded = sem("consts_loaded")
        step_loaded = sem("step_loaded")
        stored = sem("stored")
        set_up = sem("set_up")
        a_full, a_free = sem("a_full"), sem("a_free")
        v_full = sem("v_full")
        v_free = sem("v_free")
        s_full, s_max, s_exp = sem("s_full"), sem("s_max"), sem("s_exp")
        o_full, o_done = sem("o_full"), sem("o_done")
        km_ready, xv_ready, xb_ready = sem("km_ready"), sem("xv_ready"), sem("xb_ready")
        var_ready, sd_ready, xh_ready = sem("var_ready"), sem("sd_ready"), sem("xh_ready")
        rep_ready, exp4_ready, p4_ready = sem("rep_ready"), sem("exp4_ready"), sem("p4_ready")
        dve_done = sem("dve_done")

        def a_job(i, n):
            return i * A_STEP + n + 1

        def v_job(i, n):
            return i * V_STEP + n + 1

        def v_emptied(i, n):
            return i * V_STEP + n + 2

        loads = []
        for n in MATS0 + MATS1 + MATSC:
            rows = CH0 if n in MATS0 else CH1 if n in MATS1 else CHC
            for k, r in enumerate(rows):
                loads.append((w[n][0:r, k, :], d[n][sum(rows[:k]):sum(rows[:k]) + r, :]))
        loads.append((w_ff2[:, :, :], d["ff_w2"].rearrange("(t p) n -> p t n", p=128)))
        for t, n in ((w_qca, "Wq_ca"), (mask0, "mask0"), (mask1, "mask1"), (maskv, "maskv"), (bias, "bias"),
                     (ln_g, "ln_g"), (ln_b, "ln_b"), (ff_b, "ff_b")):
            src = d[n]
            loads.append((t[tuple(slice(None) for _ in src.shape)], src))
        CONSTS = 16 * len(loads)
        LOADS_STEP = 16 * 7

        block = ctx.enter_context(nc.Block())

        @block.sync
        def _(sp):
            def load_step(i):
                for k, r in enumerate(CH0):
                    sp.dma_start(xT[0:r, k, :], d["xT"][i, AT0[k]:AT0[k] + r, :]).then_inc(step_loaded, 16)
                for k, r in enumerate(CHC):
                    sp.dma_start(cT[0:r, k, :], d["cT"][i, k * r:(k + 1) * r, :]).then_inc(step_loaded, 16)
                sp.dma_start(caG[:, :], d["caG"][i, :, :]).then_inc(step_loaded, 16)
                sp.dma_start(xin[:, :, :], d["x"][i, :, :, :].rearrange("g s c -> s g c")).then_inc(step_loaded, 16)

            def store_step(i):
                for b in range(G):
                    sp.wait_ge(v_free, v_emptied(i, V_AT["y"] + b))
                    sp.dma_start(out[i, b, :, :], X[:, b, :]).then_inc(stored, 16)

            sp.dma_start(ident[:, :], d["ident"]).then_inc(stored, 16)
            load_step(0)
            for dst, src in loads:
                sp.dma_start(dst, src).then_inc(consts_loaded, 16)
            with sp.Fori(0, STEPS - 1) as i:
                sp.wait_ge(o_full, i * (ATT * G) + 2 * G)
                sp.wait_ge(var_ready, i * (3 * G) + G)
                load_step(i + 1)
                store_step(i)
            store_step(STEPS - 1)
            sp.wait_ge(stored, 16 + 16 * B)

        @block.gpsimd
        def _(pool):
            def add_bias(i, j, src):
                for b in range(G):
                    if j:
                        pool.wait_ge(xh_ready, i * (3 * G) + (j - 1) * G + b + 1)
                    nc.gpsimd.tensor_tensor(X[:, b, :], src[:, b, :], bias[:, j, :], ALU.add).then_inc(xb_ready, 1)

            def mask_keys(i, att, src, rows, heads, mask, keys):
                for b in range(G):
                    n = att * G + b
                    if n >= 2:
                        pool.wait_ge(s_full, i * UNITS_STEP + unit_of((n - 1) // G, (n - 1) % G))
                    at = 0
                    for k, r in enumerate(rows):
                        m = heads[k]
                        last = nc.gpsimd.tensor_tensor(
                            KM[0:r, n % 2, at:at + m * keys].rearrange("p (h s) -> p h s", h=m),
                            src[0:r, k, b * S:b * S + keys].unsqueeze(1).to_broadcast([r, m, keys]),
                            mask[0:r, 0:m].unsqueeze(2).to_broadcast([r, m, keys]), ALU.mult)
                        at += m * keys
                    last.then_inc(km_ready, 1)

            pool.wait_ge(consts_loaded, CONSTS)
            with pool.Fori(0, STEPS) as i:
                pool.wait_ge(v_free, i * V_STEP + 1)
                pool.wait_ge(step_loaded, i * LOADS_STEP + LOADS_STEP)
                pool.wait_ge(stored, i * (16 * G) + 16)
                add_bias(i, 0, xin)
                for b in range(G):
                    nc.gpsimd.tensor_copy(xV[:, b, :, 0:D0],
                                          xin[:, b, :].rearrange("p (h e) -> p h e", h=HEADS0)).then_inc(xv_ready, 1)
                pool.wait_ge(v_free, v_emptied(i, V_AT["K0T"] + 2))
                mask_keys(i, 0, KA, CH0, HC0, mask0, KEYS0)
                mask_keys(i, 1, xT, CH0, HC0, mask0, S)
                add_bias(i, 1, X)
                pool.wait_ge(v_free, v_emptied(i, V_AT["K1T"] + 2))
                mask_keys(i, 2, KA, CH1, HC1, mask1, S)
                add_bias(i, 2, X)
                mask_keys(i, 3, KB, CH1, HC1, mask1, S)
                add_bias(i, 3, X)

        @block.scalar
        def _(act):
            def copy_chunks(i, stage, dst, rows):
                for k, r in enumerate(rows):
                    n = A_AT[stage] + k
                    act.wait_ge(a_full, a_job(i, n))
                    nc.scalar.activation(dst[0:r, k, :], a_bank[n % 2][0:r, :], ACT.Copy).then_inc(a_free, 1)

            def copy_values(i, stage, dst, heads, e):
                for b in range(G):
                    n = A_AT[stage] + b
                    act.wait_ge(a_full, a_job(i, n))
                    nc.scalar.activation(dst[:, b, :, 0:e],
                                         a_bank[n % 2][:, 0:H].rearrange("p (h e) -> p h e", h=heads),
                                         ACT.Copy).then_inc(a_free, 1)

            def exps(i, att, keys):
                for b in range(G):
                    for u, (_, _, m) in enumerate(UNITS[att]):
                        n = unit_of(att, b, u)
                        act.wait_ge(s_max, i * UNITS_STEP + n + 1)
                        for h in range(m):
                            last = nc.scalar.activation(
                                P[:, n % 3, h * keys:(h + 1) * keys], s_bank[n % 3][:, h * keys:(h + 1) * keys],
                                ACT.Exp, bias=nmax[:, n % 3, h:h + 1])
                        last.then_inc(s_exp, 1)

            def roots(i, j):
                for b in range(G):
                    act.wait_ge(var_ready, i * (3 * G) + j * G + b + 1)
                    nc.scalar.activation(sd[:, b, :], mv[:, b, 1:2], ACT.Sqrt, bias=eps[:, 0:1]).then_inc(sd_ready, 1)

            act.wait_ge(consts_loaded, CONSTS)
            with act.Fori(0, STEPS) as i:
                act.wait_ge(v_free, i * V_STEP + 1)
                copy_chunks(i, "Q0T", QA, CH0)
                copy_chunks(i, "Q1caT", QB, CH0)
                copy_values(i, "V0", V0, HEADS0, D0)
                copy_values(i, "V2", V2, HEADS1, D1)
                exps(i, 0, KEYS0)
                exps(i, 1, S)
                copy_chunks(i, "Q2caT", QA, CH0)
                act.wait_ge(v_free, v_emptied(i, V_AT["s4"]))
                nc.scalar.activation(p4[:, :, :], p4[:, :, :], ACT.Exp).then_inc(exp4_ready, 1)
                roots(i, 0)
                copy_chunks(i, "Q1T", QB, CH1)
                copy_values(i, "V1", V1, HEADS1, D1)
                exps(i, 2, S)
                roots(i, 1)
                copy_chunks(i, "Q2T", QA, CH1)
                exps(i, 3, S)
                roots(i, 2)
                for t in range(FFT):
                    n = A_AT["gates"] + t
                    act.wait_ge(a_full, a_job(i, n))
                    if t >= 2:
                        act.wait_ge(v_free, v_emptied(i, V_AT["values"] + t - 2))
                    nc.scalar.activation(gate[:, t % 2, :], a_bank[n % 2][:, :], ACT.Gelu,
                                         bias=ff_b[:, 1, t:t + 1]).then_inc(a_free, 1)

        @block.vector
        def _(dve):
            jobs = [0]
            links = [0]

            def link(i, ins):
                links[0] += 1
                ins.then_inc(dve_done, 1)
                dve.wait_ge(dve_done, i * LINKS_STEP + links[0])

            def filled(i, stage=None):
                n = jobs[0]
                assert stage is None or n == V_AT[stage]
                jobs[0] += 1
                dve.wait_ge(v_full, v_job(i, n))
                return v_bank[n % 2]

            def copy_chunks(i, stage, dst, rows):
                for k, r in enumerate(rows):
                    bank = filled(i, stage if k == 0 else None)
                    nc.vector.tensor_copy(dst[0:r, k, :], bank[0:r, :]).then_inc(v_free, 1)

            def normalise(i, att, b, heads, e, dst):
                dve.wait_ge(o_full, i * (ATT * G) + att * G + b + 1)
                o = o_bank[:, 0:heads * (e + 1)].rearrange("p (h e) -> p h e", h=heads)
                link(i, nc.vector.reciprocal(rden[:, 0:heads].unsqueeze(2), o[:, :, e:e + 1]))
                nc.vector.tensor_tensor(dst[:, b, :].rearrange("p (h e) -> p h e", h=heads), o[:, :, 0:e],
                                        rden[:, 0:heads].unsqueeze(2).to_broadcast([128, heads, e]), ALU.mult)\
                    .then_inc(o_done, 1)

            def attention(i, att, heads, e, keys, dst):
                units = UNITS[att]
                order = [(b, u) for b in range(G) for u in range(len(units))]
                for x in range(len(order) + 2):
                    n = unit_of(att, 0) + x
                    if x < len(order):
                        m = units[order[x][1]][2]
                        dve.wait_ge(s_full, i * UNITS_STEP + n + 1)
                        nc.vector.tensor_reduce(nmax[:, n % 3, 0:m],
                                                s_bank[n % 3][:, 0:m * keys].rearrange("p (h s) -> p h s", h=m),
                                                axis=AX.X, op=ALU.max, negate=True).then_inc(s_max, 1)
                    if x >= 2:
                        m = units[order[x - 2][1]][2]
                        bank = filled(i, f"att{att}" if x == 2 else None)
                        nc.vector.tensor_copy(PT[0:keys, n % 2, 0:m * S], bank[0:keys, 0:m * S]).then_inc(v_free, 1)
                    if x >= 3 and order[x - 3][1] == len(units) - 1:
                        normalise(i, att, order[x - 3][0], heads, e, dst)
                normalise(i, att, G - 1, heads, e, dst)

            def copy_hT(i, b, rows, stage=None):
                bank = filled(i, stage)
                nc.vector.tensor_copy(hT[0:rows[0], 0:2, b * S:(b + 1) * S],
                                      bank[0:rows[0], 0:2 * S].rearrange("p (k s) -> p k s", k=2))
                nc.vector.tensor_copy(hT[0:rows[2], 2, b * S:(b + 1) * S],
                                      bank[0:rows[2], 2 * S:3 * S]).then_inc(v_free, 1)

            def project_out(i, j, rows):
                for x in range(G + 3):
                    if x < G:
                        copy_hT(i, x, rows, f"out{j}" if x == 0 else None)
                    if 1 <= x <= G:
                        b = x - 1
                        bank = filled(i)
                        dve.wait_ge(xb_ready, i * (4 * G) + j * G + b + 1)
                        nc.vector.tensor_tensor(X[:, b, :], bank[:, 0:H], X[:, b, :], ALU.add).then_inc(v_free, 1)
                        dve.wait_ge(v_free, v_emptied(i, jobs[0] - 1))
                        link(i, nc.vector.bn_stats(stats[:, b, :], X[:, b, :]))
                        nc.vector.tensor_copy(waited[:, :], eps[:, :])
                        nc.vector.bn_aggr(mv[:, b, :], stats[:, b, :]).then_inc(var_ready, 1)
                    if 2 <= x <= G + 1:
                        b = x - 2
                        dve.wait_ge(sd_ready, i * (3 * G) + j * G + b + 1)
                        link(i, nc.vector.reciprocal(sd[:, b, :], sd[:, b, :]))
                        nc.vector.tensor_scalar(XH[:, b, :], X[:, b, :], mv[:, b, 0:1], sd[:, b, :],
                                                ALU.subtract, ALU.mult).then_inc(xh_ready, 1)
                    if x >= 3:
                        b = x - 3
                        bank = filled(i)
                        for k, r in enumerate(CH1):
                            last = nc.vector.tensor_scalar(hT[0:r, k, b * S:(b + 1) * S], bank[0:r, k * S:(k + 1) * S],
                                                           ln_g[0:r, j, k:k + 1], ln_b[0:r, j, k:k + 1],
                                                           ALU.mult, ALU.add)
                        last.then_inc(v_free, 1)

            for t, e in ((xV, D0), (V0, D0), (V1, D1), (V2, D1)):
                nc.vector.memset(t[:, :, :, e:e + 1], 1.0).then_inc(set_up, 1)
            dve.wait_ge(consts_loaded, CONSTS)
            dve.wait_ge(set_up, 4)
            nc.vector.memset(eps[:, :], EPS).then_inc(v_free, 1)
            with dve.Fori(0, STEPS) as i:
                dve.wait_ge(v_free, i * V_STEP + 1)
                dve.wait_ge(step_loaded, i * LOADS_STEP + LOADS_STEP)
                for k in range(2):
                    last = nc.vector.tensor_copy(
                        carep[:, k, :, :, :],
                        cT[:, k, :].rearrange("p (b s) -> p b s", b=G)[:, :, KEYS0:S].unsqueeze(2)
                        .to_broadcast([96, G, HEADS0, T4]))
                last.then_inc(rep_ready, 1)
                copy_chunks(i, "K0T", KA, CH0)
                bank = filled(i, "kca")
                for k, r in enumerate(CH0):
                    for b in range(G):
                        src = bank[0:r, (k * G + b) * T4:(k * G + b + 1) * T4]
                        last = nc.vector.tensor_tensor(
                            kca[0:r, k, b, 0:HC0[k], :], src.unsqueeze(1).to_broadcast([r, HC0[k], T4]),
                            mask0[0:r, 0:HC0[k]].unsqueeze(2).to_broadcast([r, HC0[k], T4]), ALU.mult)
                last.then_inc(v_free, 1)
                bank = filled(i, "vca")
                nc.vector.tensor_tensor(vca[:, :], bank[:, 0:H], maskv[:, :], ALU.mult).then_inc(v_free, 1)
                copy_chunks(i, "K2T", KB, CH1)
                attention(i, 0, HEADS0, D0, KEYS0, HS)
                attention(i, 1, HEADS0, D0, S, O)
                for b in range(G):
                    copy_hT(i, b, CH0, "ca_hsT" if b == 0 else None)
                bank = filled(i, "s4")
                s4 = bank[:, 0:G * HEADS0 * T4].rearrange("p (q t) -> p q t", t=T4)
                over4 = m4[:, :].unsqueeze(2).to_broadcast([128, G * HEADS0, T4])
                link(i, nc.vector.tensor_reduce(m4[:, :], s4, axis=AX.X, op=ALU.max))
                nc.vector.tensor_tensor(p4[:, :, :], s4, over4, ALU.subtract).then_inc(v_free, 1)
                dve.wait_ge(exp4_ready, i + 1)
                link(i, nc.vector.tensor_reduce(m4[:, :], p4[:, :, :], axis=AX.X, op=ALU.add))
                link(i, nc.vector.reciprocal(m4[:, :], m4[:, :]))
                nc.vector.tensor_tensor(p4[:, :, :], p4[:, :, :], over4, ALU.mult).then_inc(p4_ready, 1)
                bank = filled(i, "p4T")
                nc.vector.tensor_copy(p4T[:, :], bank[:, 0:128]).then_inc(v_free, 1)
                for b in range(G):
                    bank = filled(i)
                    nc.vector.tensor_tensor(HS[:, b, :], bank[:, 0:H], HS[:, b, :], ALU.add).then_inc(v_free, 1)
                project_out(i, 0, CH0)
                copy_chunks(i, "K1T", KA, CH1)
                attention(i, 2, HEADS1, D1, S, O)
                project_out(i, 1, CH1)
                attention(i, 3, HEADS1, D1, S, O)
                project_out(i, 2, CH1)
                for t in range(FFT):
                    bank = filled(i, "values" if t == 0 else None)
                    dve.wait_ge(a_free, a_job(i, A_AT["gates"] + t))
                    nc.vector.scalar_tensor_tensor(out=F[:, t, :], in0=bank[:, :], scalar=ff_b[:, 0, t:t + 1],
                                                   in1=gate[:, t % 2, :], op0=ALU.add, op1=ALU.mult)\
                        .then_inc(v_free, 1)
                for b in range(G):
                    bank = filled(i, "y" if b == 0 else None)
                    dve.wait_ge(xb_ready, i * (4 * G) + 3 * G + b + 1)
                    nc.vector.tensor_tensor(X[:, b, :], bank[:, 0:H], X[:, b, :], ALU.add).then_inc(v_free, 1)
                assert jobs[0] == V_STEP and links[0] == LINKS_STEP

        @block.tensor
        def _(pe):
            a_jobs, v_jobs = [0], [0]

            def mm(o, lhsT, rhs, start=True, stop=True):
                return nc.tensor.matmul(o, lhsT, rhs, start=start, stop=stop)

            def a_next(i, stage=None):
                n = a_jobs[0]
                assert stage is None or n == A_AT[stage]
                a_jobs[0] += 1
                if n >= 2:
                    pe.wait_ge(a_free, a_job(i, n - 2))
                return a_bank[n % 2]

            def v_next(i, stage=None):
                n = v_jobs[0]
                assert stage is None or n == V_AT[stage]
                v_jobs[0] += 1
                if n >= 2:
                    pe.wait_ge(v_free, v_emptied(i, n - 2))
                return v_bank[n % 2]

            def transposed(bank, wn, rows_k, src, c, at, r):
                for k, rk in enumerate(rows_k):
                    last = mm(bank[0:r, :], w[wn][0:rk, k, at:at + r], src[0:rk, k, :], k == 0, k == len(rows_k) - 1)
                return last

            def natural(bank, wn, rows_k, src, b):
                for k, rk in enumerate(rows_k):
                    last = mm(bank[:, 0:H], src[0:rk, k, b * S:(b + 1) * S], w[wn][0:rk, k, :],
                              k == 0, k == len(rows_k) - 1)
                return last

            def blocks(bank, src, b, at, rows):
                for k, r in enumerate(rows):
                    last = nc.tensor.transpose(bank[0:r, k * S:(k + 1) * S], src[:, b, at[k]:at[k] + r], ident[:, :])
                return last

            def attention(i, att, Q, V, heads, e, keys, rows, a_ready):
                units = UNITS[att]
                hc = HC0 if heads == HEADS0 else HC1
                order = [(b, u) for b in range(G) for u in range(len(units))]
                first = unit_of(att, 0)
                pe.wait_ge(a_free, a_job(i, a_ready))
                for x in range(len(order) + 3):
                    if x < len(order):
                        b, u = order[x]
                        c, h0, m = units[u]
                        n = first + x
                        if u == 0:
                            pe.wait_ge(km_ready, i * (ATT * G) + att * G + b + 1)
                        if n >= 3:
                            pe.wait_ge(s_exp, i * UNITS_STEP + n - 2)
                        at = (sum(hc[:c]) + h0) * keys
                        mm(s_bank[n % 3][:, 0:m * keys], Q[0:rows[c], c, b * S:(b + 1) * S],
                           KM[0:rows[c], (att * G + b) % 2, at:at + m * keys]).then_inc(s_full, 1)
                    if 2 <= x < len(order) + 2:
                        m = units[order[x - 2][1]][2]
                        n = first + x - 2
                        pe.wait_ge(s_exp, i * UNITS_STEP + n + 1)
                        bank = v_next(i, f"att{att}" if x == 2 else None)
                        for h in range(m):
                            last = nc.tensor.transpose(bank[0:keys, h * S:(h + 1) * S],
                                                       P[:, n % 3, h * keys:(h + 1) * keys], ident[:, :])
                        last.then_inc(v_full, 1)
                    if x >= 3:
                        b, u = order[x - 3]
                        c, h0, m = units[u]
                        n = first + x - 3
                        pe.wait_ge(v_free, v_emptied(i, V_AT[f"att{att}"] + x - 3))
                        if u == 0 and att * G + b:
                            pe.wait_ge(o_done, i * (ATT * G) + att * G + b)
                        for h in range(m):
                            head = sum(hc[:c]) + h0 + h
                            last = mm(o_bank[:, head * (e + 1):(head + 1) * (e + 1)],
                                      PT[0:keys, n % 2, h * S:(h + 1) * S], V[0:keys, b, head, :])
                        if u == len(units) - 1:
                            last.then_inc(o_full, 1)

            def project_out(i, j, wn, src, at, rows, src_ready):
                for x in range(G + 3):
                    if x < G:
                        src_ready(x)
                        blocks(v_next(i, f"out{j}" if x == 0 else None), src, x, at, rows).then_inc(v_full, 1)
                        last_hT = v_jobs[0] - 1
                        hT_job.append(last_hT)
                    if 1 <= x <= G:
                        pe.wait_ge(v_free, v_emptied(i, hT_job[-2] if x < G else hT_job[-1]))
                        natural(v_next(i), wn, rows, hT, x - 1).then_inc(v_full, 1)
                    if x >= 3:
                        pe.wait_ge(xh_ready, i * (3 * G) + j * G + x - 2)
                        blocks(v_next(i), XH, x - 3, AT1, CH1).then_inc(v_full, 1)
                pe.wait_ge(v_free, v_emptied(i, v_jobs[0] - 1))

            hT_job = []
            pe.wait_ge(consts_loaded, CONSTS)
            pe.wait_ge(stored, 16)
            with pe.Fori(0, STEPS) as i:
                pe.wait_ge(v_free, i * V_STEP + 1)
                pe.wait_ge(step_loaded, i * LOADS_STEP + LOADS_STEP)
                for c, r in enumerate(CH0):
                    transposed(a_next(i), "Wq", CH0, xT, c, AT0[c], r).then_inc(a_full, 1)
                    transposed(v_next(i), "Wk", CHC, cT, c, AT0[c], r).then_inc(v_full, 1)
                for c, r in enumerate(CH0):
                    mm(a_next(i)[0:r, :], w_qca[:, AT0[c]:AT0[c] + r], caG[:, :]).then_inc(a_full, 1)
                bank = v_next(i, "kca")
                for c, r in enumerate(CH0):
                    for k, rk in enumerate(CHC):
                        last = mm(bank[0:r, c * G * T4:(c + 1) * G * T4], w["Wk_ca"][0:rk, k, AT0[c]:AT0[c] + r],
                                  cT[0:rk, k, :].rearrange("p (b s) -> p b s", b=G)[:, :, KEYS0:S], k == 0, k == 1)
                last.then_inc(v_full, 1)
                bank = v_next(i, "vca")
                pe.wait_ge(rep_ready, i + 1)
                for k, rk in enumerate(CHC):
                    last = mm(bank[:, 0:H], carep[0:rk, k, :, :, :].rearrange("p b h t -> p (b h t)"),
                              w["Wv_ca"][0:rk, k, :], k == 0, k == 1)
                last.then_inc(v_full, 1)
                for b in range(G):
                    natural(a_next(i), "Wv", CHC, cT, b).then_inc(a_full, 1)
                for c, r in enumerate(CH1):
                    transposed(v_next(i), "k2", CHC, cT, c, AT1[c], r).then_inc(v_full, 1)
                for b in range(G):
                    natural(a_next(i), "v2", CHC, cT, b).then_inc(a_full, 1)

                attention(i, 0, QA, V0, HEADS0, D0, KEYS0, CH0, A_AT["V0"] + G - 1)
                pe.wait_ge(xv_ready, i * G + G)
                attention(i, 1, QB, xV, HEADS0, D0, S, CH0, A_AT["Q1caT"] + 2)

                for b in range(G):
                    pe.wait_ge(o_done, i * (ATT * G) + G + b + 1)
                    blocks(v_next(i), O, b, AT0, CH0).then_inc(v_full, 1)
                pe.wait_ge(v_free, v_emptied(i, V_AT["ca_hsT"] + G - 1))
                for c, r in enumerate(CH0):
                    transposed(a_next(i, "Q2caT" if c == 0 else None), "Wq", CH0, hT, c, AT0[c], r).then_inc(a_full, 1)
                bank = v_next(i, "s4")
                pe.wait_ge(a_free, a_job(i, A_AT["Q2caT"] + 2))
                for b in range(G):
                    for c, r in enumerate(CH0):
                        at = (b * HEADS0 + sum(HC0[:c])) * T4
                        last = mm(bank[:, at:at + HC0[c] * T4], QA[0:r, c, b * S:(b + 1) * S],
                                  kca[0:r, c, b, 0:HC0[c], :].rearrange("p h t -> p (h t)"))
                last.then_inc(v_full, 1)
                pe.wait_ge(p4_ready, i + 1)
                nc.tensor.transpose(v_next(i, "p4T")[:, 0:128], p4[:, :, :].rearrange("p q t -> p (q t)"),
                                    ident[:, :]).then_inc(v_full, 1)
                pe.wait_ge(v_free, v_emptied(i, V_AT["p4T"]))
                for b in range(G):
                    rows = slice(b * HEADS0 * T4, (b + 1) * HEADS0 * T4)
                    mm(v_next(i)[:, 0:H], p4T[rows, :], vca[rows, :]).then_inc(v_full, 1)

                project_out(i, 0, "Wout", HS, AT0, CH0,
                            lambda b: pe.wait_ge(v_free, v_emptied(i, V_AT["ca_hs2"] + b)))
                for c, r in enumerate(CH1):
                    transposed(a_next(i, "Q1T" if c == 0 else None), "q1", CH1, hT, c, AT1[c], r).then_inc(a_full, 1)
                    transposed(v_next(i, "K1T" if c == 0 else None), "k1", CH1, hT, c, AT1[c], r).then_inc(v_full, 1)
                for b in range(G):
                    natural(a_next(i), "v1", CH1, hT, b).then_inc(a_full, 1)
                attention(i, 2, QB, V1, HEADS1, D1, S, CH1, A_AT["V1"] + G - 1)
                project_out(i, 1, "o1_w", O, AT1, CH1,
                            lambda b: pe.wait_ge(o_done, i * (ATT * G) + 2 * G + b + 1))
                for c, r in enumerate(CH1):
                    transposed(a_next(i, "Q2T" if c == 0 else None), "q2", CH1, hT, c, AT1[c], r).then_inc(a_full, 1)
                attention(i, 3, QA, V2, HEADS1, D1, S, CH1, A_AT["Q2T"] + 2)
                project_out(i, 2, "o2_w", O, AT1, CH1,
                            lambda b: pe.wait_ge(o_done, i * (ATT * G) + 3 * G + b + 1))
                for t in range(FFT):
                    transposed(a_next(i, "gates" if t == 0 else None), "ff_w1", CH1, hT, t, FF + t * 128, 128)\
                        .then_inc(a_full, 1)
                    transposed(v_next(i, "values" if t == 0 else None), "ff_w1", CH1, hT, t, t * 128, 128)\
                        .then_inc(v_full, 1)
                pe.wait_ge(v_free, v_emptied(i, V_AT["values"] + FFT - 1))
                for b in range(G):
                    bank = v_next(i)
                    for t in range(FFT):
                        last = mm(bank[:, 0:H], F[:, t, b * S:(b + 1) * S], w_ff2[:, t, :], t == 0, t == FFT - 1)
                    last.then_inc(v_full, 1)
                assert a_jobs[0] == A_STEP and v_jobs[0] == V_STEP


def kernel(**inputs):
    import numpy as np
    import concourse.bacc as bacc
    from concourse.bass_utils import run_bass_kernel_spmd

    p = {n.split("_xattn_")[-1]: np.ascontiguousarray(a) for n, a in inputs.items()}
    x, c = p["x"].reshape(STEPS, G, S, H), p["ctx_768"].reshape(STEPS, G, S, C)
    arrays = {
        "x": x,
        "xT": x.transpose(0, 3, 1, 2).reshape(STEPS, H, GS),
        "cT": c.transpose(0, 3, 1, 2).reshape(STEPS, C, GS),
    }
    channels = np.linspace(0, C - 1, S).astype(np.int64)
    arrays["caG"] = c[:, :, KEYS0:, :][:, :, :, channels].transpose(0, 2, 1, 3).reshape(STEPS, T4, GS)
    for n in MATS0 + MATS1 + MATSC + ("ff_w2", "Wq_ca"):
        arrays[n] = p[n]

    def chunked(v):
        out = np.zeros((128, 3), v.dtype)
        for k, r in enumerate(CH1):
            out[:r, k] = v[AT1[k]:AT1[k] + r]
        return out

    arrays["bias"] = np.broadcast_to(np.stack([p[n] for n in ("b_out", "o1_b", "o2_b", "ff_b2")]), (128, 4, H))
    arrays["ln_g"] = np.stack([chunked(p[f"n{j}_g"]) for j in (1, 2, 3)], 1)
    arrays["ln_b"] = np.stack([chunked(p[f"n{j}_b"]) for j in (1, 2, 3)], 1)
    arrays["ff_b"] = p["ff_b1"].reshape(2, FFT, 128).transpose(2, 0, 1)
    arrays["ident"] = np.eye(128, dtype=np.float32)
    arrays["mask0"] = (np.arange(120)[:, None] // D0 == np.arange(3)).astype(np.float32) * np.float32(D0 ** -0.5)
    arrays["mask1"] = (np.arange(128)[:, None] // D1 == np.arange(8)).astype(np.float32) * np.float32(D1 ** -0.5)
    arrays["maskv"] = (np.arange(128)[:, None] // T4 % HEADS0 == np.arange(H) // D0).astype(np.float32)

    nc = bacc.Bacc("TRN2", target_bir_lowering=False, num_devices=1)
    arrays = {n: np.ascontiguousarray(a) for n, a in arrays.items()}
    d = {n: nc.dram_tensor(f"in_{n}", a.shape, mybir.dt.from_np(a.dtype), kind="ExternalInput").ap()
         for n, a in arrays.items()}
    out = nc.dram_tensor("out_0", (STEPS, G, S, H), mybir.dt.float32, kind="ExternalOutput").ap()
    build(nc, d, out)
    r = run_bass_kernel_spmd(nc, [{f"in_{n}": a for n, a in arrays.items()}], core_ids=[0])
    return r.results[0]["out_0"].reshape(B, S, H)
```

```python
import concourse.bass as bass
from concourse import mybir
from contextlib import ExitStack

B, S, H, C = 64, 128, 320, 192
G = 2
STEPS = B // G
GS = G * S
T4 = 4
KEYS0 = S - T4
HEADS0, HEADS1 = 8, 20
D0, D1 = H // HEADS0, H // HEADS1
FF = 4 * H
FFT = FF // 128
EPS = 1e-5
J_BANKS = 4

CH0 = (120, 120, 80)
CH1 = (128, 128, 64)
CHC = (96, 96)
AT0, AT1 = (0, 120, 240), (0, 128, 256)
HC0, HC1 = (3, 3, 2), (8, 8, 4)

MATS0 = ("Wq", "Wout")
MATS1 = ("o1_w", "o2_w")
MATSC = ("Wk", "Wv", "Wk_ca", "Wv_ca", "k2", "v2")
MATSN = ("q1", "k1", "v1", "q2", "ff_w1")
NORM_OF = {"q1": 0, "k1": 0, "v1": 0, "q2": 1, "ff_w1": 2}

PASSES = ((0, 0, 0), (0, 1, 0), (3, 0, 0), (1, 0, 1), (1, 1, 1), (4, 0, 1), (2, 0, 2), (2, 1, 2))
P_SCALE = 16384.0
X_SCALE = 1024.0
W_EXP = 14
WAIT_BASE = 32
PV_PASSES = ((0, 0), (0, 1), (0, 2), (1, 0), (1, 1))

UNITS0 = ((0, 0, 3), (1, 0, 3), (2, 0, 2))
UNITS1 = ((0, 0, 4), (0, 4, 4), (1, 0, 4), (1, 4, 4), (2, 0, 4))
CA, FIRST, SELF, CROSS = range(4)
ATT_UNITS = (UNITS0, UNITS0, UNITS1, UNITS1)
KEYS = (S, KEYS0, S, S)
ALL_UNITS = [(att, b, u) for att in range(4) for b in range(G) for u in range(len(ATT_UNITS[att]))]
UNITS_STEP = len(ALL_UNITS)
STREAMS = ((0, 12), (12, 22), (22, 32))
CHUNKS_STEP = 4 * G * 3
KM_SLOTS = 3


def chunk_of(n):
    att, b, u = ALL_UNITS[n]
    return (att * G + b) * 3 + ATT_UNITS[att][u][0]


LAST_UNIT = {chunk_of(n): n for n in range(UNITS_STEP)}

START = [("q1ca", 3, "A"), ("Q0T", 3, "A"), ("K0T", 3, "V"), ("V0", G, "AV"), ("kca", 1, "V"), ("vca", 1, "V")]


def stream_jobs(first, end, inserts):
    jobs = []
    for x in range(first, end + 3):
        jobs += inserts.get(x, [])
        if first + 2 <= x < end + 2:
            jobs.append((f"T{x - 2}", 1, "AV"))
    return jobs


INSERTS = {7: [("caT0", 1, "V")], 10: [("caT1", 1, "V")], 11: [("Q2ca", 3, "A")], 12: [("K2T", 3, "V")],
           13: [("s4", 1, "V")], 14: [("V2", G, "AV")]}
INSERTS2 = {21: [("outT1_0", 1, "V")], 23: [("outM1_0", 1, "V")]}
INSERTS3 = {31: [("outT2_0", 1, "V")], 33: [("outM2_0", 1, "V")]}


def fft(t):
    return (f"ff{t}", 1, "AV")


WINDOW1 = [("p4T", 1, "V"), fft(0), ("hs2", G, "V"), fft(1), ("outT0_0", 1, "V"), ("outT0_1", 1, "V"), fft(2),
           ("outM0_0", 1, "V"), ("outM0_1", 1, "V"), fft(3), fft(4), ("XT0_0", 1, "AV"), ("XT0_1", 1, "AV"),
           ("K1T", 3, "V"), ("Q1T", 3, "A"), ("V1", G, "AV")]
WINDOW2 = [fft(5), ("outT1_1", 1, "V"), fft(6), ("outM1_1", 1, "V"), ("XT1_0", 1, "AV"), fft(7), fft(8),
           ("XT1_1", 1, "AV"), ("Q2T", 3, "A"), fft(9), ("y", G, "V")]
WINDOW3 = [("q1ca", 3, "A"), ("outT2_1", 1, "V"), ("Q0T", 3, "A"), ("outM2_1", 1, "V"), ("XT2_0", 1, "AV"),
           ("K0T", 3, "V"), ("V0", G, "AV"), ("XT2_1", 1, "AV"), ("kca", 1, "V"), ("vca", 1, "V")]
BODY = (stream_jobs(*STREAMS[0], INSERTS) + WINDOW1 + stream_jobs(*STREAMS[1], INSERTS2) + WINDOW2
        + stream_jobs(*STREAMS[2], INSERTS3) + WINDOW3)
TAIL = [fft(t) for t in range(FFT)] + [("y", G, "V")]


class Jobs:

    def __init__(self, table, whole=None):
        total = {who: sum(c for _, c, m in (whole or table) if who in m or who == "J") for who in "JAV"}
        mine = {who: sum(c for _, c, m in table if who in m or who == "J") for who in "JAV"}
        self.skipped = {who: total[who] - mine[who] for who in "JAV"} if whole else dict.fromkeys("JAV", 0)
        at = dict(self.skipped)
        self.at, self.mode, self.by_number = {}, {}, []
        for name, c, m in table:
            self.at[name], self.mode[name] = dict(at), m
            for k in range(c):
                self.by_number.append((m, {who: at[who] + k for who in "JAV"}))
            for who in "JAV":
                if who in m or who == "J":
                    at[who] += c
        self.total = at

    def number(self, name, k, who="J"):
        return self.at[name][who] + k


LOOP_JOBS = Jobs(BODY)
HEAD_JOBS = Jobs(START, BODY)
TAIL_JOBS = Jobs(TAIL)
PER = LOOP_JOBS.total
HEAD_LINKS, STEP_LINKS = 12, 23


def last_on_bank(jobs, n):
    if jobs is HEAD_JOBS:
        k = n - HEAD_JOBS.skipped["J"] - J_BANKS
        if k < 0:
            return None
        m, nums = HEAD_JOBS.by_number[k]
        back = 0
    elif n >= J_BANKS:
        m, nums = jobs.by_number[n - J_BANKS]
        back = 0
    else:
        at = max(k for k in range(PER["J"]) if k % J_BANKS == n % J_BANKS)
        m, nums = LOOP_JOBS.by_number[at]
        back = 1
    who = "V" if "V" in m else "A"
    return back, who, nums[who]


def build(nc, d, out):
    dt = mybir.dt
    f32, f16, bf16 = dt.float32, dt.float16, dt.bfloat16
    ALU, ACT, AX = mybir.AluOpType, mybir.ActivationFunctionType, mybir.AxisListType
    ctx, staging = ExitStack(), ExitStack()
    with ctx:
        def sb(name, shape, dtype=f32):
            return ctx.enter_context(nc.sbuf_tensor(name, shape, dtype))

        def sem(name):
            return ctx.enter_context(nc.semaphore(name))

        w = {}
        for n in MATS0 + MATS1:
            w[n] = sb("w_" + n, [128, 3, H])
        for n in MATSC:
            w[n] = sb("w_" + n, [96, 2, H])
        w_ff2 = sb("w_ff2", [128, FFT, H])
        w_qca = sb("w_qca", [T4, H])
        w16 = {n: sb("w16_" + n, [128, 2, 3, 2 * FF if n == "ff_w1" else H], f16) for n in MATSN}
        ident = sb("ident", [128, 128])
        mask0 = sb("mask0", [120, 3])
        mask1 = sb("mask1", [128, 8])
        mask_self = sb("mask_self", [128, 8])
        mask_cross = sb("mask_cross", [128, 8])
        maskv = sb("maskv", [64, H])
        bias = sb("bias", [128, 4, H])
        ln_g = sb("ln_g", [128, 3, 3])
        ln_b = sb("ln_b", [128, 3, 3])
        ff_b = sb("ff_b", [128, 2 * FFT])
        qk_b = sb("qk_b", [128, 9])
        v_b = sb("v_b", [1, H])
        one_row = sb("one_row", [1, S])
        one_col = sb("one_col", [128, 1])
        eps = sb("eps", [128, 1])
        minus_half = sb("minus_half", [128, 1])
        waited = sb("waited", [128, 1])
        primed = sb("primed", [128, 1])
        amax = sb("amax", [128, 2 * len(MATSN) + 1])
        amax_row = sb("amax_row", [1, 1])
        scale = sb("scale", [128, 3])
        V0 = sb("V0", [128, G, HEADS0, 3, D0 + 1], bf16)
        VX = sb("VX", [128, G, HEADS0, 3, D0 + 1], bf16)
        V1 = sb("V1", [128, G, HEADS1, 3, D1 + 1], bf16)
        V2 = sb("V2", [128, G, HEADS1, 3, D1 + 1], bf16)
        X3 = sb("X3", [128, G, H])
        hT3 = sb("hT3", [128, 5, GS], f16)

        raw = {n: staging.enter_context(nc.sbuf_tensor("raw_" + n, [128, 3, 2 * FF if n == "ff_w1" else H], f32))
               for n in MATSN}
        staging.close()

        xT = sb("xT", [120, 3, GS])
        cT = sb("cT", [96, 2, GS])
        caG = sb("caG", [T4, GS])
        xin = sb("xin", [128, G, H])
        HS = xin
        carep = sb("carep", [96, 2, G, HEADS0, T4])
        QA, QB = sb("QA", [128, 3, GS]), sb("QB", [128, 3, GS])
        KA, KB = sb("KA", [128, 3, GS]), sb("KB", [128, 3, GS])
        KM = sb("KM", [128, KM_SLOTS, 8 * S])
        P = sb("P", [128, 3, 4 * S])
        PT = sb("PT", [128, 2, 2, 4 * S], f16)
        nmax = sb("nmax", [128, 3, 4])
        rden = sb("rden", [128, HEADS1])
        O = sb("O", [128, G, 3 * S])
        XH = O
        vrest = sb("vrest", [128, 2, H])
        xrest = sb("xrest", [128, H])
        hT = sb("hT", [128, 3, GS])
        hTn = sb("hTn", [128, 5, GS], f16)
        kca = sb("kca", [120, 3, G, 3, T4])
        vca = sb("vca", [64, H])
        p4_wide = sb("p4", [128, S // T4, T4])
        p4 = p4_wide[:, 0:G * HEADS0, :]
        m4 = sb("m4", [128, G * HEADS0])
        p4T = sb("p4T", [64, 128])
        X = sb("X", [128, G, H])
        stats = sb("stats", [128, G, 6])
        mv = sb("mv", [128, G, 2])
        rstd = sb("rstd", [128, G, 1])
        gate = sb("gate", [128, 2, GS])
        F = sb("F", [128, FFT, GS])

        banks = [ctx.enter_context(nc.psum_tensor(f"bank{i}", [128, 512], f32)) for i in range(8)]
        s_bank, o_bank, j_bank = banks[0:3], banks[3], banks[4:8]

        consts_loaded, raw_loaded = sem("consts_loaded"), sem("raw_loaded")
        step_loaded = sem("step_loaded")
        stored = sem("stored")
        set_up, shifts_ready = sem("set_up"), sem("shifts_ready")
        amax_ready, amax_turned, amax_all = sem("amax_ready"), sem("amax_turned"), sem("amax_all")
        amax_one, scale_ready = sem("amax_one"), sem("scale_ready")
        high_ready, low_ready = sem("high_ready"), sem("low_ready")
        j_full = sem("j_full")
        a_done = sem("a_done")
        v_done = sem("v_done")
        s_full, s_max, s_exp = sem("s_full"), sem("s_max"), sem("s_exp")
        o_full, o_done = sem("o_full"), sem("o_done")
        km_ready, vx_ready, xb_ready = sem("km_ready"), sem("vx_ready"), sem("xb_ready")
        var_ready, rstd_ready, xh_ready = sem("var_ready"), sem("rstd_ready"), sem("xh_ready")
        rep_ready, exp4_ready, p4_ready = sem("rep_ready"), sem("exp4_ready"), sem("p4_ready")
        v_ready = sem("v_ready")
        dve_done, pool_done = sem("dve_done"), sem("pool_done")

        def done(i, number, who):
            return (i + 1) * PER[who] + number + 1

        loads = []
        for n in MATS0 + MATS1 + MATSC:
            rows = CH0 if n in MATS0 else CH1 if n in MATS1 else CHC
            for k, r in enumerate(rows):
                loads.append((w[n][0:r, k, :], d[n][sum(rows[:k]):sum(rows[:k]) + r, :]))
        loads.append((w_ff2[:, :, :], d["ff_w2"].rearrange("(t p) n -> p t n", p=128)))
        for t, n in ((w_qca, "Wq_ca"), (mask0, "mask0"), (mask1, "mask1"), (maskv, "maskv"), (bias, "bias"),
                     (ln_g, "ln_g"), (ff_b, "ff_b")):
            src = d[n]
            loads.append((t[tuple(slice(None) for _ in src.shape)], src))
        CONSTS = 16 * len(loads)
        raws = [(raw[n][:, :, :], d[n].rearrange("(k p) n -> p k n", p=128)) for n in MATSN]
        RAWS = 16 * len(raws)
        LOADS_STEP = 16 * 7

        block = ctx.enter_context(nc.Block())

        @block.sync
        def _(sp):
            def load_step(i):
                for k, r in enumerate(CH0):
                    sp.dma_start(xT[0:r, k, :], d["xT"][i, AT0[k]:AT0[k] + r, :]).then_inc(step_loaded, 16)
                for k, r in enumerate(CHC):
                    sp.dma_start(cT[0:r, k, :], d["cT"][i, k * r:(k + 1) * r, :]).then_inc(step_loaded, 16)
                sp.dma_start(caG[:, :], d["caG"][i, :, :]).then_inc(step_loaded, 16)
                sp.dma_start(xin[:, :, :], d["x"][i, :, :, :].rearrange("g s c -> s g c")).then_inc(step_loaded, 16)

            def load_next(i):
                sp.wait_ge(var_ready, i * (3 * G) + G)
                load_step(i + 1)

            for dst, src in raws:
                sp.dma_start(dst, src).then_inc(raw_loaded, 16)
            sp.dma_start(ident[:, :], d["ident"]).then_inc(stored, 16)
            sp.dma_start(ln_b[:, :, :], d["ln_b"]).then_inc(stored, 16)
            for dst, src in loads:
                sp.dma_start(dst, src).then_inc(consts_loaded, 16)
            sp.wait_ge(low_ready, 1)
            load_step(0)
            load_next(0)
            with sp.Fori(1, STEPS) as i:
                load_next(i)
                for b in range(G):
                    sp.wait_ge(v_done, done(i, LOOP_JOBS.number("y", b, "V"), "V"))
                    sp.dma_start(out[i - 1, b, :, :], X3[:, b, :]).then_inc(stored, 16)
            for b in range(G):
                sp.wait_ge(v_done, done(STEPS, TAIL_JOBS.number("y", b, "V"), "V"))
                sp.dma_start(out[STEPS - 1, b, :, :], X3[:, b, :]).then_inc(stored, 16)
            sp.wait_ge(stored, WAIT_BASE + 16 * B)

        @block.gpsimd
        def _(pool):
            POOL_LINKS = 3 * G + 3 * G
            links = [0]

            def link(i, ins):
                links[0] += 1
                ins.then_inc(pool_done, 1)
                pool.wait_ge(pool_done, i * POOL_LINKS + links[0])

            def add_bias(j, b, dst, src):
                nc.gpsimd.tensor_tensor(dst[:, b, :], src[:, b, :], bias[:, j, :], ALU.add).then_inc(xb_ready, 1)

            def mask_keys(i, att, b, src, rows, heads, mask):
                keys = KEYS[att]
                for k, r in enumerate(rows):
                    q = (att * G + b) * 3 + k
                    if q >= KM_SLOTS:
                        pool.wait_ge(s_full, i * UNITS_STEP + LAST_UNIT[q - KM_SLOTS] + 1)
                    m = heads[k]
                    nc.gpsimd.tensor_tensor(
                        KM[0:r, q % KM_SLOTS, 0:m * keys].rearrange("p (h s) -> p h s", h=m),
                        src[0:r, k, b * S:b * S + keys].unsqueeze(1).to_broadcast([r, m, keys]),
                        mask[0:r, 0:m].unsqueeze(2).to_broadcast([r, m, keys]), ALU.mult).then_inc(km_ready, 1)

            def x_values(i, b):
                def part(p):
                    return VX[:, b, :, p, 0:D0]
                x = xin[:, b, :].rearrange("p (h e) -> p h e", h=HEADS0)
                rest = xrest[:, :].rearrange("p (h e) -> p h e", h=HEADS0)
                ones = one_col[:, 0:1].unsqueeze(2).to_broadcast([128, HEADS0, D0])
                link(i, nc.gpsimd.tensor_copy(part(0), x))
                link(i, nc.gpsimd.tensor_tensor(rest, x, part(0), ALU.subtract))
                link(i, nc.gpsimd.tensor_tensor(part(1), rest, ones, ALU.mult))
                nc.gpsimd.tensor_tensor(part(2), rest, part(1), ALU.subtract).then_inc(vx_ready, 1)

            def norms(i, j, dst):
                for b in range(G):
                    pool.wait_ge(var_ready, i * (3 * G) + j * G + b + 1)
                    link(i, nc.gpsimd.tensor_tensor(rstd[:, b, :], mv[:, b, 1:2], eps[:, :], ALU.add))
                    nc.gpsimd.tensor_tensor(rstd[:, b, :], rstd[:, b, :], minus_half[:, :], ALU.pow)\
                        .then_inc(rstd_ready, 1)
                if dst is not None:
                    for b in range(G):
                        pool.wait_ge(xh_ready, i * (3 * G) + j * G + b + 1)
                        add_bias(j + 1, b, dst, dst)

            def last_bias(i):
                pool.wait_ge(v_done, done(i - 1, LOOP_JOBS.number("XT2_1", 0, "V"), "V"))
                for b in range(G):
                    add_bias(3, b, X3, X3)

            pool.wait_ge(consts_loaded, CONSTS)
            pool.wait_ge(v_done, PER["V"])
            with pool.Fori(0, STEPS) as i:
                links[0] = 0
                pool.wait_ge(j_full, done(i - 1, LOOP_JOBS.number("T31", 0), "J"))
                pool.wait_ge(step_loaded, i * LOADS_STEP + LOADS_STEP)
                mask_keys(i, CA, 0, xT, CH0, HC0, mask0)
                x_values(i, 0)
                mask_keys(i, CA, 1, xT, CH0, HC0, mask0)
                x_values(i, 1)
                pool.wait_ge(v_done, done(i - 1, LOOP_JOBS.number("K0T", 2, "V"), "V"))
                for b in range(G):
                    mask_keys(i, FIRST, b, KA, CH0, HC0, mask0)
                for b in range(G):
                    add_bias(0, b, X, xin)
                last_bias(i)
                norms(i, 0, X)
                pool.wait_ge(v_done, done(i, LOOP_JOBS.number("K1T", 2, "V"), "V"))
                for b in range(G):
                    mask_keys(i, SELF, b, KA, CH1, HC1, mask_self)
                norms(i, 1, X)
                for b in range(G):
                    mask_keys(i, CROSS, b, KB, CH1, HC1, mask_cross)
                norms(i, 2, None)
                assert links[0] == POOL_LINKS
            last_bias(STEPS)

        @block.scalar
        def _(act):
            def bank_of(i, jobs, name, k=0):
                n = jobs.number(name, k)
                act.wait_ge(j_full, done(i, n, "J"))
                return j_bank[n % J_BANKS]

            def copy_chunks(i, jobs, name, dst, rows, shift=None):
                for k, r in enumerate(rows):
                    bank = bank_of(i, jobs, name, k)
                    if shift is None:
                        nc.scalar.activation(dst[0:r, k, :], bank[0:r, 0:GS], ACT.Copy).then_inc(a_done, 1)
                    else:
                        nc.scalar.activation(dst[0:r, k, :], bank[0:r, 0:GS], ACT.Identity,
                                             bias=qk_b[0:r, shift + k:shift + k + 1]).then_inc(a_done, 1)

            def first_parts(i, jobs, name, dst, heads, e):
                for b in range(G):
                    bank = bank_of(i, jobs, name, b)
                    nc.scalar.activation(dst[:, b, :, 0, 0:e], bank[:, 0:H].rearrange("p (h e) -> p h e", h=heads),
                                         ACT.Copy).then_inc(a_done, 1)

            def high_blocks(i, name, dst, b):
                bank = bank_of(i, LOOP_JOBS, name)
                nc.scalar.activation(dst[:, 0:3, b * S:(b + 1) * S],
                                     bank[:, 0:3 * S].rearrange("p (k s) -> p k s", k=3), ACT.Copy,
                                     scale=X_SCALE).then_inc(a_done, 1)

            def gelu(i, jobs, t):
                bank = bank_of(i, jobs, f"ff{t}")
                if t >= 2:
                    act.wait_ge(v_done, done(i, jobs.number(f"ff{t - 2}", 0, "V"), "V"))
                nc.scalar.activation(gate[:, t % 2, :], bank[:, 0:GS], ACT.Gelu, scale=scale[:, 1:2],
                                     bias=ff_b[:, FFT + t:FFT + t + 1]).then_inc(a_done, 1)

            def stream(i, first, end, inserts):
                for x in range(first, end + 3):
                    for step in inserts.get(x, ()):
                        step()
                    if first + 2 <= x < end + 2:
                        n = x - 2
                        att, _, u = ALL_UNITS[n]
                        m, keys = ATT_UNITS[att][u][2], KEYS[att]
                        bank = bank_of(i, LOOP_JOBS, f"T{n}")
                        nc.scalar.activation(PT[0:keys, n % 2, 0, 0:m * S], bank[0:keys, 0:m * S], ACT.Copy,
                                             scale=P_SCALE).then_inc(a_done, 1)
                    if x < end:
                        att, _, u = ALL_UNITS[x]
                        m, keys = ATT_UNITS[att][u][2], KEYS[att]
                        act.wait_ge(s_max, i * UNITS_STEP + x + 1)
                        for h in range(m):
                            last = nc.scalar.activation(
                                P[:, x % 3, h * keys:(h + 1) * keys], s_bank[x % 3][:, h * keys:(h + 1) * keys],
                                ACT.Exp, bias=nmax[:, x % 3, h:h + 1])
                        last.then_inc(s_exp, 1)

            def exp4(i):
                act.wait_ge(v_done, done(i, LOOP_JOBS.number("s4", 0, "V"), "V"))
                nc.scalar.activation(p4, p4, ACT.Exp).then_inc(exp4_ready, 1)

            def start(i, jobs):
                copy_chunks(i, jobs, "q1ca", QB, CH0)
                copy_chunks(i, jobs, "Q0T", QA, CH0)
                first_parts(i, jobs, "V0", V0, HEADS0, D0)

            act.wait_ge(amax_ready, 1)
            nc.scalar.activation(primed[:, :], eps[:, :], ACT.Copy).then_inc(a_done, HEAD_JOBS.skipped["A"])
            act.wait_ge(scale_ready, 1)
            for n in MATSN:
                last = nc.scalar.activation(w16[n][:, 0, :, :], raw[n][:, :, :], ACT.Copy, scale=scale[:, 0:1])
                last.then_inc(high_ready, 1)
            act.wait_ge(low_ready, 1)
            start(-1, HEAD_JOBS)
            with act.Fori(0, STEPS) as i:
                L = LOOP_JOBS
                stream(i, *STREAMS[0], {
                    11: [lambda: copy_chunks(i, L, "Q2ca", QB, CH0)],
                    14: [lambda: first_parts(i, L, "V2", V2, HEADS1, D1),
                         lambda: exp4(i)]})
                for t in (0, 1, 2, 3, 4):
                    gelu(i, L, t)
                for b in range(G):
                    high_blocks(i, f"XT0_{b}", hTn, b)
                copy_chunks(i, L, "Q1T", QB, CH1, 3)
                first_parts(i, L, "V1", V1, HEADS1, D1)
                stream(i, *STREAMS[1], {})
                gelu(i, L, 5)
                gelu(i, L, 6)
                high_blocks(i, "XT1_0", hTn, 0)
                gelu(i, L, 7)
                gelu(i, L, 8)
                high_blocks(i, "XT1_1", hTn, 1)
                copy_chunks(i, L, "Q2T", QA, CH1, 6)
                gelu(i, L, 9)
                stream(i, *STREAMS[2], {})
                copy_chunks(i, L, "q1ca", QB, CH0)
                copy_chunks(i, L, "Q0T", QA, CH0)
                high_blocks(i, "XT2_0", hT3, 0)
                first_parts(i, L, "V0", V0, HEADS0, D0)
                high_blocks(i, "XT2_1", hT3, 1)
            for t in range(FFT):
                gelu(STEPS, TAIL_JOBS, t)

        @block.vector
        def _(dve):
            links = [0]

            def link(i, ins):
                links[0] += 1
                ins.then_inc(dve_done, 1)
                ahead = isinstance(i, int) and i < 0
                dve.wait_ge(dve_done, links[0] if ahead else HEAD_LINKS + i * STEP_LINKS + links[0])

            def bank_of(i, jobs, name, k=0):
                n = jobs.number(name, k)
                if jobs.mode[name] == "AV":
                    dve.wait_ge(a_done, done(i, jobs.number(name, k, "A"), "A"))
                else:
                    dve.wait_ge(j_full, done(i, n, "J"))
                return j_bank[n % J_BANKS]


            def copy_chunks(i, jobs, name, dst, rows, shifted=False):
                for k, r in enumerate(rows):
                    bank = bank_of(i, jobs, name, k)
                    if shifted:
                        nc.vector.tensor_scalar(dst[0:r, k, :], bank[0:r, 0:GS], qk_b[0:r, k:k + 1], None,
                                                ALU.add).then_inc(v_done, 1)
                    else:
                        nc.vector.tensor_copy(dst[0:r, k, :], bank[0:r, 0:GS]).then_inc(v_done, 1)

            def other_parts(i, jobs, name, dst, heads, e):
                for b in range(G):
                    bank = bank_of(i, jobs, name, b)
                    rest = vrest[:, b, :].rearrange("p (h e) -> p h e", h=heads)
                    nc.vector.tensor_tensor(rest, bank[:, 0:H].rearrange("p (h e) -> p h e", h=heads),
                                            dst[:, b, :, 0, 0:e], ALU.subtract).then_inc(v_done, 1)
                for b in range(G):
                    rest = vrest[:, b, :].rearrange("p (h e) -> p h e", h=heads)
                    dve.wait_ge(v_done, done(i, jobs.number(name, b, "V"), "V"))
                    link(i, nc.vector.tensor_copy(dst[:, b, :, 1, 0:e], rest))
                    nc.vector.tensor_tensor(dst[:, b, :, 2, 0:e], rest, dst[:, b, :, 1, 0:e], ALU.subtract)\
                        .then_inc(v_ready, 1)

            def copy_hT(i, name, b, rows):
                bank = bank_of(i, LOOP_JOBS, name)
                nc.vector.tensor_copy(hT[0:rows[0], 0:2, b * S:(b + 1) * S],
                                      bank[0:rows[0], 0:2 * S].rearrange("p (k s) -> p k s", k=2))
                nc.vector.tensor_copy(hT[0:rows[2], 2, b * S:(b + 1) * S],
                                      bank[0:rows[2], 2 * S:3 * S]).then_inc(v_done, 1)

            def low_blocks(i, name, dst, b):
                bank = bank_of(i, LOOP_JOBS, name)
                s = slice(b * S, (b + 1) * S)
                nc.vector.scalar_tensor_tensor(
                    out=dst[:, 3:5, s], in0=bank[:, 0:2 * S].rearrange("p (k s) -> p k s", k=2), scalar=X_SCALE,
                    in1=dst[:, 0:2, s], op0=ALU.mult, op1=ALU.subtract)
                nc.vector.scalar_tensor_tensor(
                    out=dst[64:128, 2, s], in0=bank[64:128, 2 * S:3 * S], scalar=X_SCALE,
                    in1=dst[64:128, 2, s], op0=ALU.mult, op1=ALU.subtract).then_inc(v_done, 1)

            def normalise(i, att, b):
                heads, e = (HEADS0, D0) if att in (CA, FIRST) else (HEADS1, D1)
                dst = HS if att == FIRST else O
                if att == FIRST:
                    dve.wait_ge(xb_ready, i * (4 * G) + b + 1)
                dve.wait_ge(o_full, i * (4 * G) + att * G + b + 1)
                o = o_bank[:, 0:heads * (e + 1)].rearrange("p (h e) -> p h e", h=heads)
                link(i, nc.vector.reciprocal(rden[:, 0:heads].unsqueeze(2), o[:, :, e:e + 1]))
                nc.vector.tensor_tensor(dst[:, b, 0:H].rearrange("p (h e) -> p h e", h=heads), o[:, :, 0:e],
                                        rden[:, 0:heads].unsqueeze(2).to_broadcast([128, heads, e]), ALU.mult)\
                    .then_inc(o_done, 1)

            def stream(i, first, end, inserts):
                for x in range(first, end + 3):
                    for step in inserts.get(x, ()):
                        step()
                    if x < end:
                        att, _, u = ALL_UNITS[x]
                        m, keys = ATT_UNITS[att][u][2], KEYS[att]
                        dve.wait_ge(s_full, i * UNITS_STEP + x + 1)
                        nc.vector.tensor_reduce(nmax[:, x % 3, 0:m],
                                                s_bank[x % 3][:, 0:m * keys].rearrange("p (h s) -> p h s", h=m),
                                                axis=AX.X, op=ALU.max, negate=True).then_inc(s_max, 1)
                    if first + 2 <= x < end + 2:
                        n = x - 2
                        att, _, u = ALL_UNITS[n]
                        m, keys = ATT_UNITS[att][u][2], KEYS[att]
                        bank = bank_of(i, LOOP_JOBS, f"T{n}")
                        nc.vector.scalar_tensor_tensor(
                            out=PT[0:keys, n % 2, 1, 0:m * S], in0=bank[0:keys, 0:m * S], scalar=P_SCALE,
                            in1=PT[0:keys, n % 2, 0, 0:m * S], op0=ALU.mult, op1=ALU.subtract).then_inc(v_done, 1)
                    if x >= first + 3:
                        att, b, u = ALL_UNITS[x - 3]
                        if u == len(ATT_UNITS[att]) - 1:
                            normalise(i, att, b)

            def residual(i, j, b):
                name = f"outM{j}_{b}"
                bank = bank_of(i, LOOP_JOBS, name)
                dst = X3 if j == 2 else X
                dve.wait_ge(xb_ready, i * (4 * G) + (0, 2 * G, 3 * G)[j] + b + 1)
                if j == 2 and b == 0:
                    dve.wait_ge(stored, i * (16 * G) + WAIT_BASE)
                nc.vector.tensor_tensor(dst[:, b, :], bank[:, 0:H], X[:, b, :], ALU.add).then_inc(v_done, 1)
                dve.wait_ge(v_done, done(i, LOOP_JOBS.number(name, 0, "V"), "V"))
                link(i, nc.vector.bn_stats(stats[:, b, :], dst[:, b, :]))
                nc.vector.tensor_copy(waited[:, :], eps[:, :])
                nc.vector.bn_aggr(mv[:, b, :], stats[:, b, :]).then_inc(var_ready, 1)

            def norm(i, j, b):
                src = X3 if j == 2 else X
                dve.wait_ge(rstd_ready, i * (3 * G) + j * G + b + 1)
                nc.vector.tensor_scalar(XH[:, b, 0:H], src[:, b, :], mv[:, b, 0:1], rstd[:, b, :],
                                        ALU.subtract, ALU.mult)
                nc.vector.tensor_scalar(XH[:, b, H:3 * S], src[:, b, 2 * S:H], mv[:, b, 0:1], rstd[:, b, :],
                                        ALU.subtract, ALU.mult).then_inc(xh_ready, 1)

            def ff(i, jobs, t):
                bank = bank_of(i, jobs, f"ff{t}")
                nc.vector.scalar_tensor_tensor(out=F[:, t, :], in0=bank[:, GS:2 * GS], scalar=ff_b[:, t:t + 1],
                                               in1=gate[:, t % 2, :], op0=ALU.add, op1=ALU.mult).then_inc(v_done, 1)

            def results(i, jobs, biases):
                for b in range(G):
                    bank = bank_of(i, jobs, "y", b)
                    dve.wait_ge(xb_ready, i * (4 * G) + biases + b + 1)
                    nc.vector.scalar_tensor_tensor(out=X3[:, b, :], in0=bank[:, 0:H], scalar=scale[:, 1:2],
                                                   in1=X3[:, b, :], op0=ALU.mult, op1=ALU.add).then_inc(v_done, 1)

            def repeat_tokens(i):
                dve.wait_ge(step_loaded, i * LOADS_STEP + LOADS_STEP)
                for k in range(2):
                    last = nc.vector.tensor_copy(
                        carep[:, k, :, :, :],
                        cT[:, k, :].rearrange("p (b s) -> p b s", b=G)[:, :, KEYS0:S].unsqueeze(2)
                        .to_broadcast([96, G, HEADS0, T4]))
                last.then_inc(rep_ready, 1)

            def token_keys(i, jobs):
                bank = bank_of(i, jobs, "kca")
                for k, r in enumerate(CH0):
                    for b in range(G):
                        src = bank[0:r, (k * G + b) * T4:(k * G + b + 1) * T4]
                        last = nc.vector.tensor_tensor(
                            kca[0:r, k, b, 0:HC0[k], :], src.unsqueeze(1).to_broadcast([r, HC0[k], T4]),
                            mask0[0:r, 0:HC0[k]].unsqueeze(2).to_broadcast([r, HC0[k], T4]), ALU.mult)
                last.then_inc(v_done, 1)

            def token_values(i, jobs):
                bank = bank_of(i, jobs, "vca")
                nc.vector.tensor_tensor(vca[:, :], bank[0:64, 0:H], maskv[:, :], ALU.mult).then_inc(v_done, 1)

            over4 = m4[:, :].unsqueeze(2).to_broadcast([128, G * HEADS0, T4])

            def scores4(i):
                bank = bank_of(i, LOOP_JOBS, "s4")
                s4 = bank[:, 0:G * HEADS0 * T4].rearrange("p (q t) -> p q t", t=T4)
                link(i, nc.vector.tensor_reduce(m4[:, :], s4, axis=AX.X, op=ALU.max))
                nc.vector.tensor_tensor(p4, s4, over4, ALU.subtract).then_inc(v_done, 1)

            def softmax4(i):
                dve.wait_ge(exp4_ready, i + 1)
                link(i, nc.vector.tensor_reduce(m4[:, :], p4, axis=AX.X, op=ALU.add))
                link(i, nc.vector.reciprocal(m4[:, :], m4[:, :]))
                nc.vector.tensor_tensor(p4, p4, over4, ALU.mult).then_inc(p4_ready, 1)

            nc.vector.memset(X3[:, :, :], 0.0)
            nc.vector.memset(hT3[:, :, :], 0.0)
            for t, e in ((VX, D0), (V0, D0), (V2, D1)):
                nc.vector.memset(t[:, :, :, 0, e:e + 1], 1.0)
            for t, e in ((VX, D0), (V0, D0), (V1, D1), (V2, D1)):
                nc.vector.memset(t[:, :, :, 1:3, e:e + 1], 0.0)
            nc.vector.memset(p4_wide[:, :, :], 0.0)
            nc.vector.memset(qk_b[:, :], 0.0)
            nc.vector.memset(minus_half[:, :], -0.5)
            nc.vector.memset(one_row[:, :], 1.0)
            nc.vector.memset(one_col[:, :], 1.0)
            link(-1, nc.vector.memset(eps[:, :], EPS))
            dve.wait_ge(consts_loaded, CONSTS)
            dve.wait_ge(shifts_ready, 1)
            for half, cs in ((slice(0, 64), 3), (slice(64, 128), 2)):
                nc.vector.tensor_copy(qk_b[half, :].rearrange("p (m c) -> p m c", m=3)[:, :, 0:cs],
                                      j_bank[0][half, 0:9].rearrange("p (m c) -> p m c", m=3)[:, :, 0:cs])
            nc.vector.tensor_tensor(ff_b[:, :], ff_b[:, :], j_bank[0][:, 16:16 + 2 * FFT], ALU.add)
            link(-1, nc.vector.tensor_copy(v_b[:, :], j_bank[1][0:1, 0:H]))
            for n in MATSN:
                for k in range(3):
                    last = nc.vector.tensor_scalar(raw[n][:, k, :], raw[n][:, k, :], ln_g[:, NORM_OF[n], k:k + 1],
                                                   None, ALU.mult)
            link(-1, last)
            for m, n in enumerate(MATSN):
                nc.vector.tensor_reduce(amax[:, 2 * m:2 * m + 1], raw[n][:, :, :], axis=AX.XY, op=ALU.max)
                last = nc.vector.tensor_reduce(amax[:, 2 * m + 1:2 * m + 2], raw[n][:, :, :], axis=AX.XY, op=ALU.min,
                                               negate=True)
            link(-1, last)
            M = 2 * len(MATSN)
            nc.vector.tensor_reduce(amax[:, M:M + 1], amax[:, 0:M], axis=AX.X, op=ALU.max).then_inc(amax_ready, 1)
            dve.wait_ge(amax_turned, 1)
            nc.vector.tensor_reduce(amax_row[:, :], j_bank[2][0:1, 0:128], axis=AX.X, op=ALU.max)\
                .then_inc(amax_one, 1)
            dve.wait_ge(amax_all, 1)
            link(-1, nc.vector.tensor_scalar(scale[:, 1:2], j_bank[3][:, 0:1], 2.0 ** -20, None, ALU.max))
            u32 = dt.int32
            link(-1, nc.vector.tensor_scalar(scale[:, 1:2].bitcast(u32), scale[:, 1:2].bitcast(u32), 0x7F800000, None,
                                             ALU.bitwise_and))
            link(-1, nc.vector.tensor_scalar(scale[:, 0:1].bitcast(u32), scale[:, 1:2].bitcast(u32), -1,
                                             254 << 23, ALU.mult, ALU.add))
            link(-1, nc.vector.tensor_scalar(scale[:, 0:1], scale[:, 0:1], 2.0 ** W_EXP, None, ALU.mult))
            link(-1, nc.vector.tensor_scalar(scale[:, 2:3], scale[:, 0:1], X_SCALE, None, ALU.mult))
            nc.vector.tensor_scalar(scale[:, 1:2], scale[:, 1:2], 2.0 ** -W_EXP / X_SCALE, None, ALU.mult)\
                .then_inc(scale_ready, 1)
            dve.wait_ge(scale_ready, 1)
            nc.vector.tensor_copy(V1[:, :, :, 0, D1:D1 + 1], scale[:, 2:3].unsqueeze(1).unsqueeze(1)
                                  .to_broadcast([128, G, HEADS1, 1]))
            link(-1, nc.vector.tensor_scalar(mask_cross[:, :], mask1[:, :], scale[:, 1:2], None, ALU.mult))
            nc.vector.tensor_scalar(mask_self[:, :], mask_cross[:, :], scale[:, 1:2], None, ALU.mult)
            nc.vector.tensor_scalar(qk_b[:, :], qk_b[:, :], scale[:, 2:3], None, ALU.mult)
            nc.vector.tensor_scalar(v_b[:, :], v_b[:, :], scale[0:1, 2:3], None, ALU.mult)
            nc.vector.tensor_scalar(ff_b[:, 0:FFT], ff_b[:, 0:FFT], scale[:, 2:3], None, ALU.mult).then_inc(set_up, 1)
            for m, n in enumerate(MATSN):
                dve.wait_ge(high_ready, m + 1)
                last = nc.vector.scalar_tensor_tensor(out=w16[n][:, 1, :, :], in0=raw[n][:, :, :],
                                                      scalar=scale[:, 0:1], in1=w16[n][:, 0, :, :],
                                                      op0=ALU.mult, op1=ALU.subtract)
            last.then_inc(low_ready, 1)
            dve.wait_ge(low_ready, 1)
            nc.vector.tensor_copy(waited[:, :], eps[:, :]).then_inc(v_done, HEAD_JOBS.skipped["V"])

            repeat_tokens(0)
            copy_chunks(-1, HEAD_JOBS, "K0T", KA, CH0)
            other_parts(-1, HEAD_JOBS, "V0", V0, HEADS0, D0)
            token_keys(-1, HEAD_JOBS)
            token_values(-1, HEAD_JOBS)
            assert links[0] == HEAD_LINKS, links[0]

            with dve.Fori(0, STEPS) as i:
                L = LOOP_JOBS
                links[0] = 0
                stream(i, *STREAMS[0], {
                    7: [lambda: copy_hT(i, "caT0", 0, CH0)],
                    10: [lambda: copy_hT(i, "caT1", 1, CH0)],
                    12: [lambda: copy_chunks(i, L, "K2T", KB, CH1)],
                    13: [lambda: scores4(i)],
                    14: [lambda: other_parts(i, L, "V2", V2, HEADS1, D1)]})
                softmax4(i)
                nc.vector.tensor_copy(p4T[:, :], bank_of(i, L, "p4T")[0:64, 0:128]).then_inc(v_done, 1)
                ff(i, L, 0)
                for b in range(G):
                    bank = bank_of(i, L, "hs2", b)
                    nc.vector.tensor_tensor(HS[:, b, :], bank[:, 0:H], HS[:, b, :], ALU.add).then_inc(v_done, 1)
                ff(i, L, 1)
                for b in range(G):
                    copy_hT(i, f"outT0_{b}", b, CH0)
                ff(i, L, 2)
                for b in range(G):
                    residual(i, 0, b)
                for b in range(G):
                    norm(i, 0, b)
                ff(i, L, 3)
                ff(i, L, 4)
                for b in range(G):
                    low_blocks(i, f"XT0_{b}", hTn, b)
                copy_chunks(i, L, "K1T", KA, CH1, True)
                other_parts(i, L, "V1", V1, HEADS1, D1)
                stream(i, *STREAMS[1], {
                    21: [lambda: copy_hT(i, "outT1_0", 0, CH1)],
                    23: [lambda: residual(i, 1, 0)],
                    24: [lambda: norm(i, 1, 0)]})
                ff(i, L, 5)
                copy_hT(i, "outT1_1", 1, CH1)
                ff(i, L, 6)
                residual(i, 1, 1)
                low_blocks(i, "XT1_0", hTn, 0)
                norm(i, 1, 1)
                ff(i, L, 7)
                ff(i, L, 8)
                low_blocks(i, "XT1_1", hTn, 1)
                ff(i, L, 9)
                results(i, L, G)
                stream(i, *STREAMS[2], {
                    31: [lambda: copy_hT(i, "outT2_0", 0, CH1)],
                    33: [lambda: residual(i, 2, 0)],
                    34: [lambda: norm(i, 2, 0)]})
                repeat_tokens(i + 1)
                copy_hT(i, "outT2_1", 1, CH1)
                residual(i, 2, 1)
                low_blocks(i, "XT2_0", hT3, 0)
                norm(i, 2, 1)
                copy_chunks(i, L, "K0T", KA, CH0)
                other_parts(i, L, "V0", V0, HEADS0, D0)
                low_blocks(i, "XT2_1", hT3, 1)
                token_keys(i, L)
                token_values(i, L)
                assert links[0] == STEP_LINKS, links[0]
            for t in range(FFT):
                ff(STEPS, TAIL_JOBS, t)
            results(STEPS, TAIL_JOBS, 0)

        @block.tensor
        def _(pe):
            filled = [0]

            def mm(o, lhsT, rhs, start=True, stop=True):
                return nc.tensor.matmul(o, lhsT, rhs, start=start, stop=stop)

            def j_next(i, jobs, name, k=0):
                n = jobs.number(name, k)
                assert n == filled[0], name
                filled[0] += 1
                before = last_on_bank(jobs, n)
                if before is not None:
                    back, who, number = before
                    pe.wait_ge(v_done if who == "V" else a_done, done(i - back, number, who))
                return j_bank[n % J_BANKS]

            def transposed(bank, wn, rows_k, src, at, r):
                for k, rk in enumerate(rows_k):
                    last = mm(bank[0:r, 0:GS], w[wn][0:rk, k, at:at + r], src[0:rk, k, :], k == 0,
                              k == len(rows_k) - 1)
                return last

            def transposed16(o, wn, src, at, r):
                for x, (blk, part, rows) in enumerate(PASSES):
                    last = mm(o, w16[wn][:, part, rows, at:at + r], src[:, blk, :], x == 0, x == len(PASSES) - 1)
                return last

            def natural(bank, wn, rows_k, src, b):
                for k, rk in enumerate(rows_k):
                    last = mm(bank[:, 0:H], src[0:rk, k, b * S:(b + 1) * S], w[wn][0:rk, k, :],
                              k == 0, k == len(rows_k) - 1)
                return last

            def turn(i, name, src, b, at, rows):
                bank = j_next(i, LOOP_JOBS, name)
                for k, r in enumerate(rows):
                    last = nc.tensor.transpose(bank[0:r, k * S:(k + 1) * S], src[:, b, at[k]:at[k] + r], ident[:, :])
                last.then_inc(j_full, 1)

            def v_job_done(i, jobs, name, k=0):
                pe.wait_ge(v_done, done(i, jobs.number(name, k, "V"), "V"))

            def queries_ca(i, jobs):
                for c, r in enumerate(CH0):
                    mm(j_next(i, jobs, "q1ca", c)[0:r, 0:GS], w_qca[:, AT0[c]:AT0[c] + r], caG[:, :])\
                        .then_inc(j_full, 1)

            def chunks(i, jobs, name, wn, rows_k, src, at, rows):
                for c, r in enumerate(rows):
                    transposed(j_next(i, jobs, name, c), wn, rows_k, src, at[c], r).then_inc(j_full, 1)

            def chunks16(i, name, wn, src):
                for c, r in enumerate(CH1):
                    bank = j_next(i, LOOP_JOBS, name, c)
                    transposed16(bank[0:r, 0:GS], wn, src, AT1[c], r).then_inc(j_full, 1)

            def values(i, jobs, name, wn):
                for b in range(G):
                    natural(j_next(i, jobs, name, b), wn, CHC, cT, b).then_inc(j_full, 1)

            def tokens(i, jobs):
                bank = j_next(i, jobs, "kca")
                for c, r in enumerate(CH0):
                    for k, rk in enumerate(CHC):
                        last = mm(bank[0:r, c * G * T4:(c + 1) * G * T4], w["Wk_ca"][0:rk, k, AT0[c]:AT0[c] + r],
                                  cT[0:rk, k, :].rearrange("p (b s) -> p b s", b=G)[:, :, KEYS0:S], k == 0, k == 1)
                last.then_inc(j_full, 1)
                bank = j_next(i, jobs, "vca")
                pe.wait_ge(rep_ready, i + 2)
                for k, rk in enumerate(CHC):
                    last = mm(bank[0:64, 0:H], carep[0:rk, k, :, :, :].rearrange("p b h t -> p (b h t)"),
                              w["Wv_ca"][0:rk, k, :], k == 0, k == 1)
                last.then_inc(j_full, 1)

            def stream(i, first, end, inserts, ready):
                for x in range(first, end + 3):
                    for step in inserts.get(x, ()):
                        step()
                    if x < end:
                        att, b, u = ALL_UNITS[x]
                        c, h0, m = ATT_UNITS[att][u]
                        keys = KEYS[att]
                        rows = CH0 if att in (CA, FIRST) else CH1
                        Q = QB if att in (CA, SELF) else QA
                        if b == 0 and u == 0:
                            ready[att]()
                        if h0 == 0:
                            pe.wait_ge(km_ready, i * CHUNKS_STEP + chunk_of(x) + 1)
                        if x >= 3:
                            pe.wait_ge(s_exp, i * UNITS_STEP + x - 2)
                        mm(s_bank[x % 3][:, 0:m * keys], Q[0:rows[c], c, b * S:(b + 1) * S],
                           KM[0:rows[c], chunk_of(x) % KM_SLOTS, h0 * keys:(h0 + m) * keys]).then_inc(s_full, 1)
                    if first + 2 <= x < end + 2:
                        n = x - 2
                        att, _, u = ALL_UNITS[n]
                        m, keys = ATT_UNITS[att][u][2], KEYS[att]
                        bank = j_next(i, LOOP_JOBS, f"T{n}")
                        pe.wait_ge(s_exp, i * UNITS_STEP + n + 1)
                        for h in range(m):
                            last = nc.tensor.transpose(bank[0:keys, h * S:(h + 1) * S],
                                                       P[:, n % 3, h * keys:(h + 1) * keys], ident[:, :])
                        last.then_inc(j_full, 1)
                    if x >= first + 3:
                        n = x - 3
                        att, b, u = ALL_UNITS[n]
                        c, h0, m = ATT_UNITS[att][u]
                        keys = KEYS[att]
                        V, e, hc = ((VX, D0, HC0), (V0, D0, HC0), (V1, D1, HC1), (V2, D1, HC1))[att]
                        if u == 0:
                            if att == CA:
                                pe.wait_ge(vx_ready, i * G + b + 1)
                            else:
                                pe.wait_ge(v_ready, i * (3 * G) + {FIRST: 0, CROSS: G, SELF: 2 * G}[att] + b + 1)
                            if att * G + b:
                                pe.wait_ge(o_done, i * (4 * G) + att * G + b)
                        v_job_done(i, LOOP_JOBS, f"T{n}")
                        for h in range(m):
                            head = sum(hc[:c]) + h0 + h
                            for y, (pp, vp) in enumerate(PV_PASSES):
                                last = mm(o_bank[:, head * (e + 1):(head + 1) * (e + 1)],
                                          PT[0:keys, n % 2, pp, h * S:(h + 1) * S], V[0:keys, b, head, vp, :],
                                          y == 0, y == len(PV_PASSES) - 1)
                        if u == len(ATT_UNITS[att]) - 1:
                            last.then_inc(o_full, 1)

            def queries_ready(i, name):
                return lambda: pe.wait_ge(a_done, done(i, LOOP_JOBS.number(name, 2, "A"), "A"))

            def turn_O(i, name, att, b, at, rows):
                pe.wait_ge(o_done, i * (4 * G) + att * G + b + 1)
                turn(i, name, O, b, at, rows)

            def out_proj(i, j, b, wn, rows):
                bank = j_next(i, LOOP_JOBS, f"outM{j}_{b}")
                v_job_done(i, LOOP_JOBS, f"outT{j}_{b}")
                natural(bank, wn, rows, hT, b).then_inc(j_full, 1)

            def turn_norm(i, j, b):
                pe.wait_ge(xh_ready, i * (3 * G) + j * G + b + 1)
                turn(i, f"XT{j}_{b}", XH, b, AT1, (S, S, S))

            def ff(i, jobs, t):
                if t == 0:
                    v_job_done(i - 1, LOOP_JOBS, "XT2_1")
                bank = j_next(i, jobs, f"ff{t}")
                transposed16(bank[:, 0:GS], "ff_w1", hT3, FF + t * 128, 128)
                transposed16(bank[:, GS:2 * GS], "ff_w1", hT3, t * 128, 128).then_inc(j_full, 1)

            def ff_out(i, jobs):
                for b in range(G):
                    bank = j_next(i, jobs, "y", b)
                    if b == 0:
                        v_job_done(i, jobs, f"ff{FFT - 1}")
                    for t in range(FFT):
                        last = mm(bank[:, 0:H], F[:, t, b * S:(b + 1) * S], w_ff2[:, t, :], t == 0, t == FFT - 1)
                    last.then_inc(j_full, 1)

            def queries2_ca(i):
                v_job_done(i, LOOP_JOBS, "caT1")
                chunks(i, LOOP_JOBS, "Q2ca", "Wq", CH0, hT, AT0, CH0)

            def scores4(i):
                bank = j_next(i, LOOP_JOBS, "s4")
                queries_ready(i, "Q2ca")()
                for b in range(G):
                    for c, r in enumerate(CH0):
                        at = (b * HEADS0 + sum(HC0[:c])) * T4
                        last = mm(bank[:, at:at + HC0[c] * T4], QB[0:r, c, b * S:(b + 1) * S],
                                  kca[0:r, c, b, 0:HC0[c], :].rearrange("p h t -> p (h t)"))
                last.then_inc(j_full, 1)

            pe.wait_ge(raw_loaded, RAWS)
            pe.wait_ge(stored, WAIT_BASE)
            for m, n in enumerate(("k1", "q1", "q2")):
                for c, r in enumerate(CH1):
                    for k, rk in enumerate(CH1):
                        mm(j_bank[0][0:r, m * 3 + c:m * 3 + c + 1], raw[n][0:rk, k, AT1[c]:AT1[c] + r],
                           ln_b[0:rk, NORM_OF[n], k:k + 1], k == 0, k == 2)
            for t in range(2 * FFT):
                for k, rk in enumerate(CH1):
                    mm(j_bank[0][:, 16 + t:17 + t], raw["ff_w1"][0:rk, k, t * 128:(t + 1) * 128],
                       ln_b[0:rk, 2, k:k + 1], k == 0, k == 2)
            for k, rk in enumerate(CH1):
                last = mm(j_bank[1][0:1, 0:H], ln_b[0:rk, 0, k:k + 1], raw["v1"][0:rk, k, :], k == 0, k == 2)
            last.then_inc(shifts_ready, 1)
            pe.wait_ge(amax_ready, 1)
            M = 2 * len(MATSN)
            nc.tensor.transpose(j_bank[2][0:1, 0:128], amax[:, M:M + 1], ident[:, :]).then_inc(amax_turned, 1)
            pe.wait_ge(amax_one, 1)
            mm(j_bank[3][:, 0:1], one_row[:, :], amax_row[:, :]).then_inc(amax_all, 1)
            pe.wait_ge(scale_ready, 1)
            nc.tensor.transpose(j_bank[2][0:1, 0:128], amax[:, M:M + 1], ident[:, :])\
                .then_inc(j_full, HEAD_JOBS.skipped["J"])

            pe.wait_ge(consts_loaded, CONSTS)
            pe.wait_ge(set_up, 1)
            pe.wait_ge(step_loaded, LOADS_STEP)
            filled[0] = HEAD_JOBS.skipped["J"]
            queries_ca(-1, HEAD_JOBS)
            chunks(-1, HEAD_JOBS, "Q0T", "Wq", CH0, xT, AT0, CH0)
            chunks(-1, HEAD_JOBS, "K0T", "Wk", CHC, cT, AT0, CH0)
            values(-1, HEAD_JOBS, "V0", "Wv")
            tokens(-1, HEAD_JOBS)
            pe.wait_ge(a_done, PER["A"])
            pe.wait_ge(v_done, PER["V"])

            with pe.Fori(0, STEPS) as i:
                L = LOOP_JOBS
                filled[0] = 0
                stream(i, *STREAMS[0], {
                    7: [lambda: turn_O(i, "caT0", CA, 0, AT0, CH0)],
                    10: [lambda: turn_O(i, "caT1", CA, 1, AT0, CH0)],
                    11: [lambda: queries2_ca(i)],
                    12: [lambda: chunks(i, L, "K2T", "k2", CHC, cT, AT1, CH1)],
                    13: [lambda: scores4(i)],
                    14: [lambda: values(i, L, "V2", "v2")]},
                    {CA: queries_ready(i - 1, "q1ca"), FIRST: queries_ready(i - 1, "Q0T")})
                pe.wait_ge(p4_ready, i + 1)
                nc.tensor.transpose(j_next(i, L, "p4T")[:, 0:128], p4_wide[:, :, :].rearrange("p q t -> p (q t)"),
                                    ident[:, :]).then_inc(j_full, 1)
                ff(i, L, 0)
                v_job_done(i, L, "p4T")
                for b in range(G):
                    rows = slice(b * HEADS0 * T4, (b + 1) * HEADS0 * T4)
                    mm(j_next(i, L, "hs2", b)[:, 0:H], p4T[rows, :], vca[rows, :]).then_inc(j_full, 1)
                ff(i, L, 1)
                for b in range(G):
                    v_job_done(i, L, "hs2", b)
                    turn(i, f"outT0_{b}", HS, b, AT0, CH0)
                ff(i, L, 2)
                for b in range(G):
                    out_proj(i, 0, b, "Wout", CH0)
                ff(i, L, 3)
                ff(i, L, 4)
                for b in range(G):
                    turn_norm(i, 0, b)
                v_job_done(i, L, "XT0_1")
                chunks16(i, "K1T", "k1", hTn)
                chunks16(i, "Q1T", "q1", hTn)
                for b in range(G):
                    bank = j_next(i, L, "V1", b)
                    for x, (blk, part, rows) in enumerate(PASSES):
                        mm(bank[:, 0:H], hTn[:, blk, b * S:(b + 1) * S], w16["v1"][:, part, rows, :], x == 0, False)
                    mm(bank[:, 0:H], one_row[:, :], v_b[:, :], False, True).then_inc(j_full, 1)
                stream(i, *STREAMS[1], {
                    21: [lambda: turn_O(i, "outT1_0", SELF, 0, AT1, CH1)],
                    23: [lambda: out_proj(i, 1, 0, "o1_w", CH1)]},
                    {SELF: queries_ready(i, "Q1T")})
                ff(i, L, 5)
                turn_O(i, "outT1_1", SELF, 1, AT1, CH1)
                ff(i, L, 6)
                out_proj(i, 1, 1, "o1_w", CH1)
                turn_norm(i, 1, 0)
                ff(i, L, 7)
                ff(i, L, 8)
                turn_norm(i, 1, 1)
                v_job_done(i, L, "XT1_1")
                chunks16(i, "Q2T", "q2", hTn)
                ff(i, L, 9)
                ff_out(i, L)
                stream(i, *STREAMS[2], {
                    31: [lambda: turn_O(i, "outT2_0", CROSS, 0, AT1, CH1)],
                    33: [lambda: out_proj(i, 2, 0, "o2_w", CH1)]},
                    {CROSS: queries_ready(i, "Q2T")})
                pe.wait_ge(step_loaded, i * LOADS_STEP + 2 * LOADS_STEP)
                queries_ca(i, L)
                turn_O(i, "outT2_1", CROSS, 1, AT1, CH1)
                chunks(i, L, "Q0T", "Wq", CH0, xT, AT0, CH0)
                out_proj(i, 2, 1, "o2_w", CH1)
                turn_norm(i, 2, 0)
                chunks(i, L, "K0T", "Wk", CHC, cT, AT0, CH0)
                values(i, L, "V0", "Wv")
                turn_norm(i, 2, 1)
                tokens(i, L)
                assert filled[0] == PER["J"]
            filled[0] = 0
            for t in range(FFT):
                ff(STEPS, TAIL_JOBS, t)
            ff_out(STEPS, TAIL_JOBS)


def kernel(**inputs):
    import numpy as np
    import concourse.bacc as bacc
    from concourse.bass_utils import run_bass_kernel_spmd

    p = {n.split("_xattn_")[-1]: np.ascontiguousarray(a) for n, a in inputs.items()}
    x, c = (np.concatenate([a, a[:1]]) for a in
            (p["x"].reshape(STEPS, G, S, H), p["ctx_768"].reshape(STEPS, G, S, C)))
    arrays = {
        "x": x,
        "xT": x.transpose(0, 3, 1, 2).reshape(STEPS + 1, H, GS),
        "cT": c.transpose(0, 3, 1, 2).reshape(STEPS + 1, C, GS),
    }
    channels = np.linspace(0, C - 1, S).astype(np.int64)
    arrays["caG"] = c[:, :, KEYS0:, :][:, :, :, channels].transpose(0, 2, 1, 3).reshape(STEPS + 1, T4, GS)
    for n in MATS0 + MATS1 + MATSC + ("ff_w2", "Wq_ca"):
        arrays[n] = p[n]
    for n in MATSN:
        arrays[n] = np.concatenate([p[n], p[n][AT1[2]:]])

    def chunked(v):
        out = np.zeros((128, 3), v.dtype)
        for k, r in enumerate(CH1):
            out[:r, k] = v[AT1[k]:AT1[k] + r]
        out[64:, 2] = v[AT1[2]:]
        return out

    arrays["bias"] = np.broadcast_to(np.stack([p[n] for n in ("b_out", "o1_b", "o2_b", "ff_b2")]), (128, 4, H))
    arrays["ln_g"] = np.stack([chunked(p[f"n{j}_g"]) for j in (1, 2, 3)], 1)
    arrays["ln_b"] = np.stack([chunked(p[f"n{j}_b"]) for j in (1, 2, 3)], 1)
    arrays["ff_b"] = p["ff_b1"].reshape(2 * FFT, 128).T
    arrays["ident"] = np.eye(128, dtype=np.float32)
    arrays["mask0"] = (np.arange(120)[:, None] // D0 == np.arange(3)).astype(np.float32) * np.float32(D0 ** -0.5)
    arrays["mask1"] = (np.arange(128)[:, None] // D1 == np.arange(8)).astype(np.float32) * np.float32(D1 ** -0.5)
    arrays["maskv"] = (np.arange(64)[:, None] // T4 % HEADS0 == np.arange(H) // D0).astype(np.float32)

    nc = bacc.Bacc("TRN2", target_bir_lowering=False, num_devices=1)
    arrays = {n: np.ascontiguousarray(a) for n, a in arrays.items()}
    d = {n: nc.dram_tensor(f"in_{n}", a.shape, mybir.dt.from_np(a.dtype), kind="ExternalInput").ap()
         for n, a in arrays.items()}
    out = nc.dram_tensor("out_0", (STEPS, G, S, H), mybir.dt.float32, kind="ExternalOutput").ap()
    build(nc, d, out)
    r = run_bass_kernel_spmd(nc, [{f"in_{n}": a for n, a in arrays.items()}], core_ids=[0])
    return r.results[0]["out_0"].reshape(B, S, H)
```

```python
import concourse.bass as bass
from concourse import mybir
from contextlib import ExitStack

B, S, H, C = 64, 128, 320, 192
G = 2
STEPS = B // G
GS = G * S
T4 = 4
KEYS0 = S - T4
HEADS0, HEADS1 = 8, 20
D0, D1 = H // HEADS0, H // HEADS1
FF = 4 * H
FFT = FF // 128
EPS = 1e-5
J_BANKS = 4

CH0 = (120, 120, 80)
CH1 = (128, 128, 64)
CHC = (96, 96)
AT0, AT1 = (0, 120, 240), (0, 128, 256)
HC0, HC1 = (3, 3, 2), (8, 8, 4)

MATS0 = ("Wq",)
MATSC = ("Wk", "Wv", "Wk_ca", "Wv_ca", "k2", "v2")
MATSN = ("q1", "k1", "v1", "q2", "ff_w1", "Wout", "o1_w", "o2_w")
NORM_OF = {"q1": 0, "k1": 0, "v1": 0, "q2": 1, "ff_w1": 2, "Wout": 3, "o1_w": 3, "o2_w": 3}

PASSES = ((0, 0, 0), (0, 1, 0), (3, 0, 0), (1, 0, 1), (1, 1, 1), (4, 0, 1), (2, 0, 2), (2, 1, 2))
P_SCALE = 16384.0
X_SCALE = 1024.0
W_EXP = 14
WAIT_BASE = 48
PV_PASSES = ((0, 0), (0, 1), (1, 0))
V_EXP = 14
FX, F0, F2, F1 = range(4)
OUT_COLUMN = (0, 2, 1)

UNITS0 = ((0, 0, 3), (1, 0, 3), (2, 0, 2))
UNITS1 = ((0, 0, 4), (0, 4, 4), (1, 0, 4), (1, 4, 4), (2, 0, 4))
CA, FIRST, SELF, CROSS = range(4)
ATT_UNITS = (UNITS0, UNITS0, UNITS1, UNITS1)
KEYS = (S, KEYS0, S, S)
ALL_UNITS = [(att, b, u) for att in range(4) for b in range(G) for u in range(len(ATT_UNITS[att]))]
UNITS_STEP = len(ALL_UNITS)
STREAMS = ((0, 12), (12, 22), (22, 32))
CHUNKS_STEP = 4 * G * 3
KM_SLOTS = 3


def chunk_of(n):
    att, b, u = ALL_UNITS[n]
    return (att * G + b) * 3 + ATT_UNITS[att][u][0]


LAST_UNIT = {chunk_of(n): n for n in range(UNITS_STEP)}

START = [("q1ca", 3, "A"), ("Q0T", 3, "A"), ("K0T", 3, "V"), ("mT", 1, "V"), ("mB", 1, "V")]


def stream_jobs(first, end, pre=None, mid=None, post=None):
    jobs = []
    for x in range(first, end + 3):
        jobs += (pre or {}).get(x, [])
        jobs += (mid or {}).get(x, [])
        if first + 2 <= x < end + 2:
            jobs.append((f"T{x - 2}", 1, "AV"))
        jobs += (post or {}).get(x, [])
    return jobs


def fft(t):
    return (f"ff{t}", 1, "AV")


def one(name, who):
    return (name, 1, who)


PRE1 = {4: [one("vca", "V")], 5: [one("XT2_1", "AV")], 7: [one("caT0", "V")], 10: [one("caT1", "V")], 11: [("Q2ca", 3, "A")],
        12: [one("s4", "V")], 14: [fft(1)]}
MID1 = {2: [one("kca", "V")]}
POST1 = {6: [one("V0_0", "AV")], 9: [one("V0_1", "AV")], 12: [fft(0)]}
WINDOW1 = [fft(2), one("p4T", "V"), fft(3), ("hs2", G, "V"), fft(4), one("outT0_0", "AV"), one("outT0_1", "AV"), fft(5),
           one("outM0_0", "V"), one("outM0_1", "V"), fft(6), fft(7), one("XT0_0", "AV"), fft(8), one("XT0_1", "AV"),
           fft(9), ("K1T", 3, "V"), one("V1_0", "AV"), one("V1_1", "AV"), ("Q1T", 3, "A")]
PRE2 = {22: [one("outT1_0", "AV")], 23: [one("V2_1", "AV")], 24: [one("K2T0", "V"), one("outM1_0", "V")]}
POST2 = {20: [one("V2_0", "AV")]}
WINDOW2 = [one("K2T1", "V"), one("K2T2", "V"), one("outT1_1", "AV"), one("y0", "V"),
           one("outM1_1", "V"), one("XT1_0", "AV"), one("XT1_1", "AV"), one("y1", "V"), one("Q2T0", "A"),
           one("mT", "V"), one("Q2T1", "A"), one("mB", "V"), one("Q2T2", "A")]
PRE3 = {32: [one("outT2_0", "AV"), one("K0T1", "V")], 33: [one("Q0T0", "A")], 34: [one("outM2_0", "V")]}
POST3 = {30: [one("K0T0", "V")]}
WINDOW3 = [("q1ca", 3, "A"), one("Q0T1", "A"), one("outT2_1", "AV"), one("K0T2", "V"), one("outM2_1", "V"),
           one("XT2_0", "AV"), one("Q0T2", "A")]
BODY = (stream_jobs(*STREAMS[0], PRE1, MID1, POST1) + WINDOW1 + stream_jobs(*STREAMS[1], PRE2, None, POST2) + WINDOW2
        + stream_jobs(*STREAMS[2], PRE3, None, POST3) + WINDOW3)
TAIL = [one("XT2_1", "AV")] + [fft(t) for t in range(FFT)] + [one("y0", "V"), one("y1", "V")]


class Jobs:

    def __init__(self, table, whole=None):
        total = {who: sum(c for _, c, m in (whole or table) if who in m or who == "J") for who in "JAV"}
        mine = {who: sum(c for _, c, m in table if who in m or who == "J") for who in "JAV"}
        self.skipped = {who: total[who] - mine[who] for who in "JAV"} if whole else dict.fromkeys("JAV", 0)
        at = dict(self.skipped)
        self.at, self.mode, self.by_number = {}, {}, []
        for name, c, m in table:
            self.at[name], self.mode[name] = dict(at), m
            for k in range(c):
                self.by_number.append((m, {who: at[who] + k for who in "JAV"}))
            for who in "JAV":
                if who in m or who == "J":
                    at[who] += c
        self.total = at

    def number(self, name, k=0, who="J"):
        if name not in self.at and name[:-1] in self.at:
            name, k = name[:-1], int(name[-1])
        return self.at[name][who] + k


class Order:

    def __init__(self, who):
        self.who, self.next = who, 0

    def restart(self, n=0):
        self.next = n

    def take(self, jobs, name, k=0):
        assert jobs.number(name, k, self.who) == self.next, (self.who, name, k, self.next)
        self.next += 1


LOOP_JOBS = Jobs(BODY)
HEAD_JOBS = Jobs(START, BODY)
TAIL_JOBS = Jobs(TAIL)
PER = LOOP_JOBS.total
HEAD_LINKS, STEP_LINKS = 19, 25


def last_on_bank(jobs, n):
    if jobs is HEAD_JOBS:
        k = n - HEAD_JOBS.skipped["J"] - J_BANKS
        if k < 0:
            return None
        m, nums = HEAD_JOBS.by_number[k]
        back = 0
    elif n >= J_BANKS:
        m, nums = jobs.by_number[n - J_BANKS]
        back = 0
    else:
        at = max(k for k in range(PER["J"]) if k % J_BANKS == n % J_BANKS)
        m, nums = LOOP_JOBS.by_number[at]
        back = 1
    who = "V" if "V" in m else "A"
    return back, who, nums[who]


def build(nc, d, out):
    dt = mybir.dt
    f32, f16 = dt.float32, dt.float16
    ALU, ACT, AX = mybir.AluOpType, mybir.ActivationFunctionType, mybir.AxisListType
    ctx, staging = ExitStack(), ExitStack()
    with ctx:
        def sb(name, shape, dtype=f32):
            return ctx.enter_context(nc.sbuf_tensor(name, shape, dtype))

        def sem(name):
            return ctx.enter_context(nc.semaphore(name))

        w = {}
        for n in MATS0:
            w[n] = sb("w_" + n, [128, 3, H])
        for n in MATSC:
            w[n] = sb("w_" + n, [96, 2, H])
        w_ff2 = sb("w_ff2", [128, FFT, H])
        w_qca = sb("w_qca", [T4, H])
        w16 = {n: sb("w16_" + n, [128, 2, 3, 2 * FF if n == "ff_w1" else H], f16) for n in MATSN}
        ident = sb("ident", [128, 128])
        mask0 = sb("mask0", [120, 3])
        mask1 = sb("mask1", [128, 8])
        mask_self = sb("mask_self", [128, 8])
        mask_cross = sb("mask_cross", [128, 8])
        maskv = sb("maskv", [64, H])
        bias = sb("bias", [128, 4, H])
        ln_g = sb("ln_g", [128, 4, 3])
        ln_b = sb("ln_b", [128, 3, 3])
        ff_b = sb("ff_b", [128, 2 * FFT])
        qk_b = sb("qk_b", [128, 9])
        v_b = sb("v_b", [1, H])
        one_row = sb("one_row", [1, S])
        one_col = sb("one_col", [128, 1])
        eps = sb("eps", [128, 1])
        minus_half = sb("minus_half", [128, 1])
        waited = sb("waited", [128, 1])
        primed = sb("primed", [128, 1])
        amax = sb("amax", [128, len(MATSN), 2, 3])
        amax_one_each = sb("amax_one_each", [128, 3])
        gains = sb("gains", [128, 4, 3])
        amax_row = sb("amax_row", [1, 1])
        scale = sb("scale", [128, 3])
        V0 = sb("V0", [128, G, HEADS0, 2, D0 + 1], f16)
        VX = sb("VX", [128, G, HEADS0, 2, D0 + 1], f16)
        V1 = sb("V1", [128, G, HEADS1, 2, D1 + 1], f16)
        V2 = sb("V2", [128, G, HEADS1, 2, D1 + 1], f16)
        X3 = sb("X3", [128, G, H])
        hT3 = sb("hT3", [128, 5, GS], f16)

        ext_wide = sb("ext_wide", [128, 128])
        ones_square = sb("ones_square", [128, 128])
        emax = sb("emax", [128, 1])
        diag = sb("diag", [128, 14])
        sizes = sb("sizes", [128, 7])
        bound_mul, bound_add = sb("bound_mul", [128, 4]), sb("bound_add", [128, 4])
        factor = sb("factor", [128, 4])
        out_factor = sb("out_factor", [128, 3])
        out_inverse = sb("out_inverse", [128, 3])
        one1 = sb("one1", [128, 1])
        p4_wide = sb("p4", [128, S // T4, T4])

        raw = {n: staging.enter_context(nc.sbuf_tensor("raw_" + n, [128, 3, 2 * FF if n == "ff_w1" else H], f32))
               for n in MATSN}
        staging.close()

        xT = sb("xT", [120, 3, GS])
        cT = sb("cT", [96, 2, GS])
        caG = sb("caG", [T4, GS])
        xin = sb("xin", [128, G, H])
        HS = xin
        carep = sb("carep", [96, 2, G, HEADS0, T4])
        QA, QB = sb("QA", [128, 3, GS]), sb("QB", [128, 3, GS])
        KA, KB = sb("KA", [128, 3, GS]), sb("KB", [128, 3, GS])
        KM = sb("KM", [128, KM_SLOTS, 8 * S])
        P = sb("P", [128, 3, 4 * S])
        PT = sb("PT", [128, 2, 2, 4 * S], f16)
        nmax = sb("nmax", [128, 3, 4])
        rden = sb("rden", [128, HEADS1])
        O = sb("O", [128, G, 3 * S])
        XH = O
        xrest = sb("xrest", [128, G, H])
        hT = sb("hT", [128, 3, GS])
        hTn = sb("hTn", [128, 5, GS], f16)
        kca = sb("kca", [120, 3, G, 3, T4])
        vca = sb("vca", [64, H])
        p4 = p4_wide[:, 0:G * HEADS0, :]
        m4 = sb("m4", [128, G * HEADS0])
        p4T = sb("p4T", [64, 128])
        X = sb("X", [128, G, H])
        stats = sb("stats", [128, G, 6])
        mv = sb("mv", [128, G, 2])
        rstd = sb("rstd", [128, G, 1])
        gate = sb("gate", [128, 2, GS])
        F = sb("F", [128, FFT, GS])

        banks = [ctx.enter_context(nc.psum_tensor(f"bank{i}", [128, 512], f32)) for i in range(8)]
        s_bank, o_bank, j_bank = banks[0:3], banks[3], banks[4:8]

        consts_loaded = sem("consts_loaded")
        raw_loaded = {n: sem("raw_loaded_" + n) for n in MATSN}
        step_loaded = sem("step_loaded")
        stored = sem("stored")
        shifts_ready = sem("shifts_ready")
        amax_ready, amax_turned, amax_all = sem("amax_ready"), sem("amax_turned"), sem("amax_all")
        amax_one, scale_ready = sem("amax_one"), sem("scale_ready")
        high_ready, low_ready = sem("high_ready"), sem("low_ready")
        j_full = sem("j_full")
        a_done = sem("a_done")
        v_done = sem("v_done")
        s_full, s_max, s_exp = sem("s_full"), sem("s_max"), sem("s_exp")
        o_full, o_done = sem("o_full"), sem("o_done")
        km_ready, vx_ready, xb_ready = sem("km_ready"), sem("vx_ready"), sem("xb_ready")
        var_ready, rstd_ready, xh_ready = sem("var_ready"), sem("rstd_ready"), sem("xh_ready")
        rep_ready, exp4_ready, p4_ready = sem("rep_ready"), sem("exp4_ready"), sem("p4_ready")
        ext_ready, diag_ready, factor_ready = sem("ext_ready"), sem("diag_ready"), sem("factor_ready")
        dve_done, pool_done = sem("dve_done"), sem("pool_done")

        def done(i, number, who):
            return (i + 1) * PER[who] + number + 1

        loads = []
        for n in MATS0 + MATSC:
            rows = CH0 if n in MATS0 else CHC
            for k, r in enumerate(rows):
                loads.append((w[n][0:r, k, :], d[n][sum(rows[:k]):sum(rows[:k]) + r, :]))
        loads.append((w_ff2[:, :, :], d["ff_w2"].rearrange("(t p) n -> p t n", p=128)))
        for t, n in ((w_qca, "Wq_ca"), (mask0, "mask0"), (mask1, "mask1"), (maskv, "maskv"), (bias, "bias"),
                     (ff_b, "ff_b")):
            src = d[n]
            loads.append((t[tuple(slice(None) for _ in src.shape)], src))
        CONSTS = 16 * len(loads)
        LOADS_STEP = 16 * 7

        block = ctx.enter_context(nc.Block())

        @block.sync
        def _(sp):
            def load_step(i):
                for k, r in enumerate(CH0):
                    sp.dma_start(xT[0:r, k, :], d["xT"][i, AT0[k]:AT0[k] + r, :]).then_inc(step_loaded, 16)
                for k, r in enumerate(CHC):
                    sp.dma_start(cT[0:r, k, :], d["cT"][i, k * r:(k + 1) * r, :]).then_inc(step_loaded, 16)
                sp.dma_start(caG[:, :], d["caG"][i, :, :]).then_inc(step_loaded, 16)
                sp.dma_start(xin[:, :, :], d["x"][i, :, :, :].rearrange("g s c -> s g c")).then_inc(step_loaded, 16)

            def load_next(i):
                sp.wait_ge(v_done, done(i, LOOP_JOBS.number("K2T2", 0, "V"), "V"))
                load_step(i + 1)

            for dst, n in ((ident[:, :], "ident"), (ln_b[:, :, :], "ln_b"), (ln_g[:, :, :], "ln_g")):
                sp.dma_start(dst, d[n]).then_inc(stored, 16)
            for n in MATSN:
                sp.dma_start(raw[n][:, :, :], d[n].rearrange("(k p) n -> p k n", p=128)).then_inc(raw_loaded[n], 16)
            for dst, src in loads:
                sp.dma_start(dst, src).then_inc(consts_loaded, 16)
            sp.wait_ge(low_ready, 1)
            load_step(0)
            load_next(0)
            with sp.Fori(1, STEPS) as i:
                load_next(i)
                for b in range(G):
                    sp.wait_ge(v_done, done(i, LOOP_JOBS.number(f"y{b}", 0, "V"), "V"))
                    sp.dma_start(out[i - 1, b, :, :], X3[:, b, :]).then_inc(stored, 16)
            for b in range(G):
                sp.wait_ge(v_done, done(STEPS, TAIL_JOBS.number(f"y{b}", 0, "V"), "V"))
                sp.dma_start(out[STEPS - 1, b, :, :], X3[:, b, :]).then_inc(stored, 16)
            sp.wait_ge(stored, WAIT_BASE + 16 * B)

        @block.gpsimd
        def _(pool):
            POOL_HEAD_LINKS = 2 * G
            POOL_LINKS = 2 * G + 3 * G
            links = [0]

            def link(i, ins):
                links[0] += 1
                ins.then_inc(pool_done, 1)
                ahead = isinstance(i, int)
                pool.wait_ge(pool_done, links[0] if ahead else i * POOL_LINKS + POOL_HEAD_LINKS + links[0])

            def add_bias(j, b, dst, src):
                nc.gpsimd.tensor_tensor(dst[:, b, :], src[:, b, :], bias[:, j, :], ALU.add).then_inc(xb_ready, 1)

            def mask_keys(i, att, b, src, rows, heads, mask):
                keys = KEYS[att]
                for k, r in enumerate(rows):
                    q = (att * G + b) * 3 + k
                    if q >= KM_SLOTS:
                        pool.wait_ge(s_full, i * UNITS_STEP + LAST_UNIT[q - KM_SLOTS] + 1)
                    if att == CROSS and b == 0:
                        pool.wait_ge(v_done, done(i, LOOP_JOBS.number(f"K2T{k}", 0, "V"), "V"))
                    m = heads[k]
                    nc.gpsimd.tensor_tensor(
                        KM[0:r, q % KM_SLOTS, 0:m * keys].rearrange("p (h s) -> p h s", h=m),
                        src[0:r, k, b * S:b * S + keys].unsqueeze(1).to_broadcast([r, m, keys]),
                        mask[0:r, 0:m].unsqueeze(2).to_broadcast([r, m, keys]), ALU.mult).then_inc(km_ready, 1)

            def x_values(i, b):
                def part(p):
                    return VX[:, b, :, p, 0:D0]
                x = xin[:, b, :].rearrange("p (h e) -> p h e", h=HEADS0)
                scaled = xrest[:, b, :].rearrange("p (h e) -> p h e", h=HEADS0)
                ones = one_col[:, 0:1].unsqueeze(2)
                factors = factor[:, FX:FX + 1].unsqueeze(2)
                nc.gpsimd.tensor_tensor(VX[:, b, :, 0, D0:D0 + 1], ones.to_broadcast([128, HEADS0, 1]),
                                        factors.to_broadcast([128, HEADS0, 1]), ALU.mult)
                link(i, nc.gpsimd.tensor_tensor(scaled, x, factors.to_broadcast([128, HEADS0, D0]), ALU.mult))
                link(i, nc.gpsimd.tensor_tensor(part(0), scaled, ones.to_broadcast([128, HEADS0, D0]), ALU.mult))
                nc.gpsimd.tensor_tensor(part(1), scaled, part(0), ALU.subtract).then_inc(vx_ready, 1)

            def deviation(i, j, b):
                pool.wait_ge(var_ready, i * (3 * G) + j * G + b + 1)
                link(i, nc.gpsimd.tensor_tensor(rstd[:, b, :], mv[:, b, 1:2], eps[:, :], ALU.add))
                nc.gpsimd.tensor_tensor(rstd[:, b, :], rstd[:, b, :], minus_half[:, :], ALU.pow)\
                    .then_inc(rstd_ready, 1)

            def norms(i, j):
                for b in range(G):
                    deviation(i, j, b)
                for b in range(G):
                    pool.wait_ge(xh_ready, i * (3 * G) + j * G + b + 2)
                    add_bias(j + 1, b, X, X)

            def last_bias(i, jobs):
                pool.wait_ge(v_done, done(i, jobs.number("XT2_1", 0, "V"), "V"))
                for b in range(G):
                    add_bias(3, b, X3, X3)

            pool.wait_ge(consts_loaded, CONSTS)
            pool.wait_ge(v_done, PER["V"])
            pool.wait_ge(step_loaded, LOADS_STEP)
            pool.wait_ge(factor_ready, 1)
            for b in range(G):
                x_values(-1, b)
            mask_keys(0, CA, 0, xT, CH0, HC0, mask0)
            assert links[0] == POOL_HEAD_LINKS
            with pool.Fori(0, STEPS) as i:
                links[0] = 0
                mask_keys(i, CA, 1, xT, CH0, HC0, mask0)
                pool.wait_ge(v_done, done(i - 1, LOOP_JOBS.number("K0T2", 0, "V"), "V"))
                for b in range(G):
                    mask_keys(i, FIRST, b, KA, CH0, HC0, mask0)
                for b in range(G):
                    add_bias(0, b, X, xin)
                last_bias(i, LOOP_JOBS)
                norms(i, 0)
                pool.wait_ge(v_done, done(i, LOOP_JOBS.number("K1T", 2, "V"), "V"))
                for b in range(G):
                    mask_keys(i, SELF, b, KA, CH1, HC1, mask_self)
                norms(i, 1)
                for b in range(G):
                    mask_keys(i, CROSS, b, KB, CH1, HC1, mask_cross)
                pool.wait_ge(step_loaded, i * LOADS_STEP + 2 * LOADS_STEP)
                pool.wait_ge(factor_ready, i + 2)
                for b in range(G):
                    x_values(i, b)
                deviation(i, 2, 0)
                pool.wait_ge(s_full, i * UNITS_STEP + UNITS_STEP)
                mask_keys(i + 1, CA, 0, xT, CH0, HC0, mask0)
                deviation(i, 2, 1)
                assert links[0] == POOL_LINKS
            last_bias(STEPS, TAIL_JOBS)

        @block.scalar
        def _(act):
            order = Order("A")

            def bank_of(i, jobs, name, k=0):
                order.take(jobs, name, k)
                n = jobs.number(name, k)
                act.wait_ge(j_full, done(i, n, "J"))
                return j_bank[n % J_BANKS]

            def copy_chunk(i, jobs, name, k, dst, rows, shift=None):
                bank = bank_of(i, jobs, name, 0 if name[-1].isdigit() else k)
                r = rows[k]
                if shift is None:
                    nc.scalar.activation(dst[0:r, k, :], bank[0:r, 0:GS], ACT.Copy).then_inc(a_done, 1)
                else:
                    nc.scalar.activation(dst[0:r, k, :], bank[0:r, 0:GS], ACT.Identity,
                                         bias=qk_b[0:r, shift + k:shift + k + 1]).then_inc(a_done, 1)

            def copy_chunks(i, jobs, name, dst, rows, shift=None):
                for k in range(3):
                    copy_chunk(i, jobs, name, k, dst, rows, shift)

            def first_part(i, name, b, dst, heads, e, f):
                bank = bank_of(i, LOOP_JOBS, f"{name}_{b}")
                nc.scalar.activation(dst[:, b, :, 0, 0:e], bank[:, 0:H].rearrange("p (h e) -> p h e", h=heads),
                                     ACT.Copy, scale=factor[:, f:f + 1]).then_inc(a_done, 1)

            def high_blocks(i, name, dst, b, jobs=LOOP_JOBS, scaled=X_SCALE):
                bank = bank_of(i, jobs, name)
                nc.scalar.activation(dst[:, 0:3, b * S:(b + 1) * S],
                                     bank[:, 0:3 * S].rearrange("p (k s) -> p k s", k=3), ACT.Copy,
                                     scale=scaled).then_inc(a_done, 1)

            def high_out(i, j, b):
                c = OUT_COLUMN[j]
                high_blocks(i, f"outT{j}_{b}", hTn, b, scaled=out_factor[:, c:c + 1])

            def gelu(i, jobs, t):
                bank = bank_of(i, jobs, f"ff{t}")
                if t >= 2:
                    act.wait_ge(v_done, done(i, jobs.number(f"ff{t - 2}", 0, "V"), "V"))
                nc.scalar.activation(gate[:, t % 2, :], bank[:, 0:GS], ACT.Gelu, scale=scale[:, 1:2],
                                     bias=ff_b[:, FFT + t:FFT + t + 1]).then_inc(a_done, 1)

            def stream(i, first, end, pre, post):
                for x in range(first, end + 3):
                    for step in pre.get(x, ()):
                        step()
                    if first + 2 <= x < end + 2:
                        n = x - 2
                        att, _, u = ALL_UNITS[n]
                        m, keys = ATT_UNITS[att][u][2], KEYS[att]
                        bank = bank_of(i, LOOP_JOBS, f"T{n}")
                        nc.scalar.activation(PT[0:keys, n % 2, 0, 0:m * S], bank[0:keys, 0:m * S], ACT.Copy,
                                             scale=P_SCALE).then_inc(a_done, 1)
                    if x < end:
                        att, _, u = ALL_UNITS[x]
                        m, keys = ATT_UNITS[att][u][2], KEYS[att]
                        act.wait_ge(s_max, i * UNITS_STEP + x + 1)
                        for h in range(m):
                            last = nc.scalar.activation(
                                P[:, x % 3, h * keys:(h + 1) * keys], s_bank[x % 3][:, h * keys:(h + 1) * keys],
                                ACT.Exp, bias=nmax[:, x % 3, h:h + 1])
                        last.then_inc(s_exp, 1)
                    for step in post.get(x, ()):
                        step()

            def load_exp_table():
                nc.scalar.activation(primed[:, :], eps[:, :], ACT.Exp)

            def exp4(i):
                act.wait_ge(v_done, done(i, LOOP_JOBS.number("s4", 0, "V"), "V"))
                nc.scalar.activation(p4, p4, ACT.Exp).then_inc(exp4_ready, 1)

            act.wait_ge(amax_ready, 1)
            nc.scalar.activation(primed[:, :], eps[:, :], ACT.Copy).then_inc(a_done, HEAD_JOBS.skipped["A"])
            act.wait_ge(scale_ready, 1)
            for n in MATSN:
                for k in range(3):
                    nc.scalar.activation(w16[n][:, 0, k, :], raw[n][:, k, :], ACT.Copy,
                                         scale=gains[:, NORM_OF[n], k:k + 1]).then_inc(high_ready, 1)
            act.wait_ge(low_ready, 1)
            order.restart(HEAD_JOBS.skipped["A"])
            copy_chunks(-1, HEAD_JOBS, "q1ca", QB, CH0)
            copy_chunks(-1, HEAD_JOBS, "Q0T", QA, CH0)
            with act.Fori(0, STEPS) as i:
                L = LOOP_JOBS
                order.restart()
                act.wait_ge(factor_ready, i + 1)
                stream(i, *STREAMS[0], {
                    5: [lambda: high_blocks(i, "XT2_1", hT3, 1)],
                    11: [lambda: copy_chunks(i, L, "Q2ca", QB, CH0)],
                    12: [lambda: exp4(i)],
                    14: [lambda: gelu(i, L, 1)]}, {
                    6: [lambda: first_part(i, "V0", 0, V0, HEADS0, D0, F0)],
                    9: [lambda: first_part(i, "V0", 1, V0, HEADS0, D0, F0)],
                    12: [lambda: gelu(i, L, 0)]})
                for t in range(2, 5):
                    gelu(i, L, t)
                for b in range(G):
                    high_out(i, 0, b)
                for t in range(5, 8):
                    gelu(i, L, t)
                high_blocks(i, "XT0_0", hTn, 0)
                gelu(i, L, 8)
                high_blocks(i, "XT0_1", hTn, 1)
                gelu(i, L, 9)
                load_exp_table()
                for b in range(G):
                    first_part(i, "V1", b, V1, HEADS1, D1, F1)
                copy_chunks(i, L, "Q1T", QB, CH1, 3)
                stream(i, *STREAMS[1], {22: [lambda: high_out(i, 1, 0)],
                                        23: [lambda: first_part(i, "V2", 1, V2, HEADS1, D1, F2)]},
                       {20: [lambda: first_part(i, "V2", 0, V2, HEADS1, D1, F2)]})
                high_out(i, 1, 1)
                high_blocks(i, "XT1_0", hTn, 0)
                high_blocks(i, "XT1_1", hTn, 1)
                for c in range(3):
                    copy_chunk(i, L, f"Q2T{c}", c, QA, CH1, 6)
                stream(i, *STREAMS[2], {32: [lambda: high_out(i, 2, 0)],
                                        33: [lambda: copy_chunk(i, L, "Q0T0", 0, QA, CH0)]}, {})
                copy_chunks(i, L, "q1ca", QB, CH0)
                copy_chunk(i, L, "Q0T1", 1, QA, CH0)
                high_out(i, 2, 1)
                high_blocks(i, "XT2_0", hT3, 0)
                copy_chunk(i, L, "Q0T2", 2, QA, CH0)
                assert order.next == PER["A"]
            order.restart()
            high_blocks(STEPS, "XT2_1", hT3, 1, TAIL_JOBS)
            for t in range(FFT):
                gelu(STEPS, TAIL_JOBS, t)

        @block.vector
        def _(dve):
            order = Order("V")
            links = [0]

            def link(i, ins):
                links[0] += 1
                ins.then_inc(dve_done, 1)
                ahead = isinstance(i, int) and i < 0
                dve.wait_ge(dve_done, links[0] if ahead else HEAD_LINKS + i * STEP_LINKS + links[0])

            def bank_of(i, jobs, name, k=0):
                order.take(jobs, name, k)
                n = jobs.number(name, k)
                if jobs.mode[name] == "AV":
                    dve.wait_ge(a_done, done(i, jobs.number(name, k, "A"), "A"))
                else:
                    dve.wait_ge(j_full, done(i, n, "J"))
                return j_bank[n % J_BANKS]


            def copy_chunk(i, jobs, name, k, dst, rows, shifted=False):
                bank = bank_of(i, jobs, name, 0 if name[-1].isdigit() else k)
                r = rows[k]
                if shifted:
                    nc.vector.tensor_scalar(dst[0:r, k, :], bank[0:r, 0:GS], qk_b[0:r, k:k + 1], None,
                                            ALU.add).then_inc(v_done, 1)
                else:
                    nc.vector.tensor_copy(dst[0:r, k, :], bank[0:r, 0:GS]).then_inc(v_done, 1)

            def copy_chunks(i, jobs, name, dst, rows, shifted=False):
                for k in range(3):
                    copy_chunk(i, jobs, name, k, dst, rows, shifted)

            def low_part(i, name, b, dst, heads, e, f):
                bank = bank_of(i, LOOP_JOBS, f"{name}_{b}")
                nc.vector.scalar_tensor_tensor(
                    out=dst[:, b, :, 1, 0:e], in0=bank[:, 0:H].rearrange("p (h e) -> p h e", h=heads),
                    scalar=factor[:, f:f + 1], in1=dst[:, b, :, 0, 0:e], op0=ALU.mult, op1=ALU.subtract)\
                    .then_inc(v_done, 1)

            def ones_column(dst, heads, e, one):
                nc.vector.tensor_copy(dst[:, :, :, 0, e:e + 1], one.unsqueeze(1).unsqueeze(1)
                                      .to_broadcast([128, G, heads, 1]))

            def extremes(rows, c, src, axis):
                nc.vector.tensor_reduce(ext_wide[0:rows, c:c + 1], src, axis=axis, op=ALU.max)
                return nc.vector.tensor_reduce(ext_wide[0:rows, c + 1:c + 2], src, axis=axis, op=ALU.min, negate=True)

            def extremes_x(i):
                dve.wait_ge(step_loaded, i * LOADS_STEP + LOADS_STEP)
                extremes(128, 0, xin[:, :, :], AX.XY)

            def extremes_context(i):
                link(i - 1, extremes(96, 2, cT[:, :, :], AX.XY))
                nc.vector.tensor_copy(ext_wide[0:96, 4:6], ext_wide[0:96, 2:4]).then_inc(ext_ready, 1)

            def diagonal(i, jobs):
                bank = bank_of(i, jobs, "mT")
                nc.vector.tensor_reduce(emax[:, :], bank[:, 0:128], axis=AX.X, op=ALU.max).then_inc(v_done, 1)
                dve.wait_ge(v_done, done(i, jobs.number("mT", 0, "V"), "V"))
                nc.vector.tensor_scalar(diag[:, :], ident[:, 0:14], emax[:, 0:1], None, ALU.mult)\
                    .then_inc(diag_ready, 1)

            def factors(i, jobs):
                bank = bank_of(i, jobs, "mB")
                pairs = bank[:, 0:14].rearrange("p (q t) -> p q t", t=2)
                nc.vector.tensor_reduce(sizes[:, :], pairs, axis=AX.X, op=ALU.max).then_inc(v_done, 1)
                dve.wait_ge(v_done, done(i, jobs.number("mB", 0, "V"), "V"))
                if jobs is HEAD_JOBS:
                    link(i, nc.vector.tensor_tensor(sizes[:, 4:5], sizes[:, 4:5], sizes[:, 6:7], ALU.max))
                    link(i, nc.vector.tensor_scalar(bound_mul[:, F0:F2 + 1], sizes[:, 4:6], 2.0 * C, None, ALU.mult))
                bits = factor[:, :].bitcast(dt.int32)
                link(i, nc.vector.tensor_tensor(factor[:, :], sizes[:, 0:4], bound_mul[:, :], ALU.mult))
                link(i, nc.vector.tensor_tensor(factor[:, :], factor[:, :], bound_add[:, :], ALU.add))
                link(i, nc.vector.tensor_scalar(bits, bits, 0x7F800000, None, ALU.bitwise_and))
                link(i, nc.vector.tensor_scalar(bits, bits, -1, 254 << 23, ALU.mult, ALU.add))
                nc.vector.tensor_scalar(factor[:, :], factor[:, :], 2.0 ** V_EXP, None, ALU.mult)\
                    .then_inc(factor_ready, 1)

            def copy_hT(i, name, b, rows):
                bank = bank_of(i, LOOP_JOBS, name)
                nc.vector.tensor_copy(hT[0:rows[0], 0:2, b * S:(b + 1) * S],
                                      bank[0:rows[0], 0:2 * S].rearrange("p (k s) -> p k s", k=2))
                nc.vector.tensor_copy(hT[0:rows[2], 2, b * S:(b + 1) * S],
                                      bank[0:rows[2], 2 * S:3 * S]).then_inc(v_done, 1)

            def low_blocks(i, name, dst, b, jobs=LOOP_JOBS, scaled=X_SCALE):
                bank = bank_of(i, jobs, name)
                s = slice(b * S, (b + 1) * S)
                nc.vector.scalar_tensor_tensor(
                    out=dst[:, 3:5, s], in0=bank[:, 0:2 * S].rearrange("p (k s) -> p k s", k=2), scalar=scaled,
                    in1=dst[:, 0:2, s], op0=ALU.mult, op1=ALU.subtract)
                nc.vector.scalar_tensor_tensor(
                    out=dst[64:128, 2, s], in0=bank[64:128, 2 * S:3 * S],
                    scalar=scaled if isinstance(scaled, float) else scaled[64:128, :],
                    in1=dst[64:128, 2, s], op0=ALU.mult, op1=ALU.subtract).then_inc(v_done, 1)

            def low_out(i, j, b):
                c = OUT_COLUMN[j]
                low_blocks(i, f"outT{j}_{b}", hTn, b, scaled=out_factor[:, c:c + 1])

            def output_factors(i):
                nc.vector.tensor_copy(out_factor[:, 0:2], factor[:, F0:F2 + 1])
                link(i, nc.vector.tensor_copy(out_factor[:, 2:3], one1[:, :]))
                link(i, nc.vector.tensor_scalar(out_inverse[:, :].bitcast(dt.int32), out_factor[:, :].bitcast(dt.int32),
                                                -1, 254 << 23, ALU.mult, ALU.add))
                link(i, nc.vector.tensor_scalar(out_inverse[:, :], out_inverse[:, :], scale[:, 1:2], X_SCALE,
                                                ALU.mult, ALU.mult))

            def normalise(i, att, b):
                heads, e = (HEADS0, D0) if att in (CA, FIRST) else (HEADS1, D1)
                dst = HS if att == FIRST else O
                if att == FIRST:
                    dve.wait_ge(xb_ready, i * (4 * G) + b + 1)
                dve.wait_ge(o_full, i * (4 * G) + att * G + b + 1)
                o = o_bank[:, 0:heads * (e + 1)].rearrange("p (h e) -> p h e", h=heads)
                link(i, nc.vector.reciprocal(rden[:, 0:heads].unsqueeze(2), o[:, :, e:e + 1]))
                last = nc.vector.tensor_tensor(
                    dst[:, b, 0:H].rearrange("p (h e) -> p h e", h=heads), o[:, :, 0:e],
                    rden[:, 0:heads].unsqueeze(2).to_broadcast([128, heads, e]), ALU.mult)
                if att in (SELF, CROSS):
                    h4 = heads - 64 // e
                    last = nc.vector.tensor_tensor(
                        dst[:, b, H:3 * S].rearrange("p (h e) -> p h e", e=e), o[:, h4:heads, 0:e],
                        rden[:, h4:heads].unsqueeze(2).to_broadcast([128, heads - h4, e]), ALU.mult)
                last.then_inc(o_done, 1)

            def stream(i, first, end, pre, mid, post):
                for x in range(first, end + 3):
                    for step in pre.get(x, ()):
                        step()
                    if x < end:
                        att, _, u = ALL_UNITS[x]
                        m, keys = ATT_UNITS[att][u][2], KEYS[att]
                        dve.wait_ge(s_full, i * UNITS_STEP + x + 1)
                        nc.vector.tensor_reduce(nmax[:, x % 3, 0:m],
                                                s_bank[x % 3][:, 0:m * keys].rearrange("p (h s) -> p h s", h=m),
                                                axis=AX.X, op=ALU.max, negate=True).then_inc(s_max, 1)
                    for step in mid.get(x, ()):
                        step()
                    if first + 2 <= x < end + 2:
                        n = x - 2
                        att, _, u = ALL_UNITS[n]
                        m, keys = ATT_UNITS[att][u][2], KEYS[att]
                        bank = bank_of(i, LOOP_JOBS, f"T{n}")
                        nc.vector.scalar_tensor_tensor(
                            out=PT[0:keys, n % 2, 1, 0:m * S], in0=bank[0:keys, 0:m * S], scalar=P_SCALE,
                            in1=PT[0:keys, n % 2, 0, 0:m * S], op0=ALU.mult, op1=ALU.subtract).then_inc(v_done, 1)
                    for step in post.get(x, ()):
                        step()
                    if x >= first + 3:
                        att, b, u = ALL_UNITS[x - 3]
                        if u == len(ATT_UNITS[att]) - 1:
                            normalise(i, att, b)

            def residual(i, j, b):
                name = f"outM{j}_{b}"
                bank = bank_of(i, LOOP_JOBS, name)
                dst = X3 if j == 2 else X
                dve.wait_ge(xb_ready, i * (4 * G) + (0, 2 * G, 3 * G)[j] + b + 1)
                if j == 2 and b == 0:
                    dve.wait_ge(stored, i * (16 * G) + WAIT_BASE)
                c = OUT_COLUMN[j]
                nc.vector.scalar_tensor_tensor(out=dst[:, b, :], in0=bank[:, 0:H], scalar=out_inverse[:, c:c + 1],
                                               in1=X[:, b, :], op0=ALU.mult, op1=ALU.add).then_inc(v_done, 1)
                dve.wait_ge(v_done, done(i, LOOP_JOBS.number(name, 0, "V"), "V"))
                link(i, nc.vector.bn_stats(stats[:, b, :], dst[:, b, :]))
                nc.vector.tensor_copy(waited[:, :], eps[:, :])
                nc.vector.bn_aggr(mv[:, b, :], stats[:, b, :]).then_inc(var_ready, 1)

            def norm(i, j, b):
                src = X3 if j == 2 else X
                dve.wait_ge(rstd_ready, i * (3 * G) + j * G + b + 1)
                nc.vector.tensor_scalar(XH[:, b, 0:H], src[:, b, :], mv[:, b, 0:1], rstd[:, b, :],
                                        ALU.subtract, ALU.mult)
                nc.vector.tensor_scalar(XH[:, b, H:3 * S], src[:, b, 2 * S:H], mv[:, b, 0:1], rstd[:, b, :],
                                        ALU.subtract, ALU.mult).then_inc(xh_ready, 1)

            def ff(i, jobs, t):
                bank = bank_of(i, jobs, f"ff{t}")
                nc.vector.scalar_tensor_tensor(out=F[:, t, :], in0=bank[:, GS:2 * GS], scalar=ff_b[:, t:t + 1],
                                               in1=gate[:, t % 2, :], op0=ALU.add, op1=ALU.mult).then_inc(v_done, 1)

            def result(i, jobs, b, biases):
                bank = bank_of(i, jobs, f"y{b}")
                dve.wait_ge(xb_ready, i * (4 * G) + biases + b + 1)
                nc.vector.scalar_tensor_tensor(out=X3[:, b, :], in0=bank[:, 0:H], scalar=scale[:, 1:2],
                                               in1=X3[:, b, :], op0=ALU.mult, op1=ALU.add).then_inc(v_done, 1)

            def repeat_tokens(i):
                dve.wait_ge(step_loaded, i * LOADS_STEP + LOADS_STEP)
                for k in range(2):
                    last = nc.vector.tensor_copy(
                        carep[:, k, :, :, :],
                        cT[:, k, :].rearrange("p (b s) -> p b s", b=G)[:, :, KEYS0:S].unsqueeze(2)
                        .to_broadcast([96, G, HEADS0, T4]))
                last.then_inc(rep_ready, 1)

            def token_keys(i, jobs):
                bank = bank_of(i, jobs, "kca")
                for k, r in enumerate(CH0):
                    for b in range(G):
                        src = bank[0:r, (k * G + b) * T4:(k * G + b + 1) * T4]
                        last = nc.vector.tensor_tensor(
                            kca[0:r, k, b, 0:HC0[k], :], src.unsqueeze(1).to_broadcast([r, HC0[k], T4]),
                            mask0[0:r, 0:HC0[k]].unsqueeze(2).to_broadcast([r, HC0[k], T4]), ALU.mult)
                last.then_inc(v_done, 1)

            def token_values(i, jobs):
                bank = bank_of(i, jobs, "vca")
                nc.vector.tensor_tensor(vca[:, :], bank[0:64, 0:H], maskv[:, :], ALU.mult).then_inc(v_done, 1)

            over4 = m4[:, :].unsqueeze(2).to_broadcast([128, G * HEADS0, T4])

            def scores4(i):
                bank = bank_of(i, LOOP_JOBS, "s4")
                s4 = bank[:, 0:G * HEADS0 * T4].rearrange("p (q t) -> p q t", t=T4)
                link(i, nc.vector.tensor_reduce(m4[:, :], s4, axis=AX.X, op=ALU.max))
                nc.vector.tensor_tensor(p4, s4, over4, ALU.subtract).then_inc(v_done, 1)

            def softmax4(i):
                dve.wait_ge(exp4_ready, i + 1)
                link(i, nc.vector.tensor_reduce(m4[:, :], p4, axis=AX.X, op=ALU.add))
                link(i, nc.vector.reciprocal(m4[:, :], m4[:, :]))
                nc.vector.tensor_tensor(p4, p4, over4, ALU.mult).then_inc(p4_ready, 1)

            nc.vector.memset(X3[:, :, :], 0.0)
            nc.vector.memset(hT3[:, :, :], 0.0)
            for t, e in ((VX, D0), (V0, D0), (V1, D1), (V2, D1)):
                nc.vector.memset(t[:, :, :, 1, e:e + 1], 0.0)
            nc.vector.memset(p4_wide[:, :, :], 0.0)
            nc.vector.memset(qk_b[:, :], 0.0)
            nc.vector.memset(minus_half[:, :], -0.5)
            nc.vector.memset(one_row[:, :], 1.0)
            nc.vector.memset(one_col[:, :], 1.0)
            nc.vector.memset(ones_square[:, :], 1.0)
            nc.vector.memset(ext_wide[:, :], 0.0)
            nc.vector.memset(bound_mul[:, :], 1.0)
            nc.vector.memset(bound_add[:, 0:3], 2.0 ** -40)
            nc.vector.memset(bound_add[:, F1:F1 + 1], 1.01 * H * X_SCALE * 2.0 ** (W_EXP + 1))
            link(-1, nc.vector.memset(eps[:, :], EPS))
            dve.wait_ge(stored, WAIT_BASE)
            for m, n in enumerate(MATSN):
                dve.wait_ge(raw_loaded[n], 16)
                nc.vector.tensor_reduce(amax[:, m, 0, :], raw[n][:, :, :], axis=AX.X, op=ALU.max)
                last = nc.vector.tensor_reduce(amax[:, m, 1, :], raw[n][:, :, :], axis=AX.X, op=ALU.min)
            link(-1, last)
            for m, n in enumerate(MATSN):
                last = nc.vector.tensor_tensor(amax[:, m, :, :], amax[:, m, :, :],
                                               ln_g[:, NORM_OF[n], :].unsqueeze(1).to_broadcast([128, 2, 3]), ALU.mult)
            link(-1, last)
            every = amax[:, :, :, :].rearrange("p m x k -> p (m x k)")
            nc.vector.tensor_reduce(amax_one_each[:, 0:1], every, axis=AX.X, op=ALU.max)
            link(-1, nc.vector.tensor_reduce(amax_one_each[:, 1:2], every, axis=AX.X, op=ALU.min, negate=True))
            nc.vector.tensor_tensor(amax_one_each[:, 2:3], amax_one_each[:, 0:1], amax_one_each[:, 1:2], ALU.max)\
                .then_inc(amax_ready, 1)
            dve.wait_ge(amax_turned, 1)
            nc.vector.tensor_reduce(amax_row[:, :], j_bank[2][0:1, 0:128], axis=AX.X, op=ALU.max)\
                .then_inc(amax_one, 1)
            dve.wait_ge(amax_all, 1)
            link(-1, nc.vector.tensor_scalar(scale[:, 1:2], j_bank[3][:, 0:1], 2.0 ** -20, None, ALU.max))
            u32 = dt.int32
            link(-1, nc.vector.tensor_scalar(scale[:, 1:2].bitcast(u32), scale[:, 1:2].bitcast(u32), 0x7F800000, None,
                                             ALU.bitwise_and))
            link(-1, nc.vector.tensor_scalar(scale[:, 0:1].bitcast(u32), scale[:, 1:2].bitcast(u32), -1,
                                             254 << 23, ALU.mult, ALU.add))
            link(-1, nc.vector.tensor_scalar(scale[:, 0:1], scale[:, 0:1], 2.0 ** W_EXP, None, ALU.mult))
            nc.vector.tensor_scalar(gains[:, :, :], ln_g[:, :, :], scale[:, 0:1], None, ALU.mult)
            link(-1, nc.vector.tensor_scalar(scale[:, 2:3], scale[:, 0:1], X_SCALE, None, ALU.mult))
            nc.vector.tensor_scalar(scale[:, 1:2], scale[:, 1:2], 2.0 ** -W_EXP / X_SCALE, None, ALU.mult)\
                .then_inc(scale_ready, 1)
            dve.wait_ge(scale_ready, 1)
            for m, n in enumerate(MATSN):
                for k in range(3):
                    dve.wait_ge(high_ready, 3 * m + k + 1)
                    nc.vector.scalar_tensor_tensor(out=w16[n][:, 1, k, :], in0=raw[n][:, k, :],
                                                   scalar=gains[:, NORM_OF[n], k:k + 1], in1=w16[n][:, 0, k, :],
                                                   op0=ALU.mult, op1=ALU.subtract)
            dve.wait_ge(consts_loaded, CONSTS)
            dve.wait_ge(shifts_ready, 1)
            for half, cs in ((slice(0, 64), 3), (slice(64, 128), 2)):
                nc.vector.tensor_copy(qk_b[half, :].rearrange("p (m c) -> p m c", m=3)[:, :, 0:cs],
                                      j_bank[0][half, 0:9].rearrange("p (m c) -> p m c", m=3)[:, :, 0:cs])
            nc.vector.tensor_tensor(ff_b[:, :], ff_b[:, :], j_bank[0][:, 16:16 + 2 * FFT], ALU.add)
            link(-1, nc.vector.tensor_copy(v_b[:, :], j_bank[1][0:1, 0:H]))
            link(-1, nc.vector.tensor_scalar(mask_cross[:, :], mask1[:, :], scale[:, 1:2], None, ALU.mult))
            nc.vector.tensor_scalar(mask_self[:, :], mask_cross[:, :], scale[:, 1:2], None, ALU.mult)
            nc.vector.tensor_scalar(qk_b[:, :], qk_b[:, :], scale[:, 2:3], None, ALU.mult)
            nc.vector.tensor_scalar(v_b[:, :], v_b[:, :], scale[0:1, 2:3], None, ALU.mult)
            nc.vector.tensor_scalar(ff_b[:, 0:FFT], ff_b[:, 0:FFT], scale[:, 2:3], None, ALU.mult)\
                .then_inc(low_ready, 1)
            dve.wait_ge(low_ready, 1)
            nc.vector.tensor_copy(waited[:, :], eps[:, :]).then_inc(v_done, HEAD_JOBS.skipped["V"])

            nc.vector.memset(XH[:, :, :], 0.0).then_inc(xh_ready, 1)
            order.restart(HEAD_JOBS.skipped["V"])
            extremes(1, 6, v_b[:, :], AX.X)
            extremes(96, 8, w["Wv"][:, :, :], AX.XY)
            extremes(96, 10, w["v2"][:, :, :], AX.XY)
            extremes(96, 12, w["Wv_ca"][:, :, :], AX.XY)
            copy_chunks(-1, HEAD_JOBS, "K0T", KA, CH0)
            extremes_x(0)
            extremes_context(0)
            diagonal(-1, HEAD_JOBS)
            factors(-1, HEAD_JOBS)
            dve.wait_ge(factor_ready, 1)
            link(-1, nc.vector.tensor_tensor(one1[:, :], factor[:, F1:F1 + 1], scale[:, 2:3], ALU.mult))
            ones_column(V1, HEADS1, D1, one1[:, 0:1])
            assert links[0] == HEAD_LINKS, links[0]

            with dve.Fori(0, STEPS) as i:
                L = LOOP_JOBS
                links[0] = 0
                order.restart()
                stream(i, *STREAMS[0], {
                    4: [lambda: token_values(i, L)],
                    5: [lambda: low_blocks(i, "XT2_1", hT3, 1)],
                    7: [lambda: copy_hT(i, "caT0", 0, CH0)],
                    10: [lambda: copy_hT(i, "caT1", 1, CH0)],
                    12: [lambda: scores4(i)],
                    14: [lambda: softmax4(i), lambda: ff(i, L, 1)]}, {
                    0: [lambda: repeat_tokens(i)],
                    1: [lambda: ones_column(V0, HEADS0, D0, factor[:, F0:F0 + 1])],
                    2: [lambda: token_keys(i, L)]}, {
                    6: [lambda: low_part(i, "V0", 0, V0, HEADS0, D0, F0)],
                    9: [lambda: low_part(i, "V0", 1, V0, HEADS0, D0, F0)],
                    12: [lambda: ff(i, L, 0)]})
                ones_column(V2, HEADS1, D1, factor[:, F2:F2 + 1])
                output_factors(i)
                ff(i, L, 2)
                nc.vector.tensor_copy(p4T[:, :], bank_of(i, L, "p4T")[0:64, 0:128]).then_inc(v_done, 1)
                ff(i, L, 3)
                for b in range(G):
                    bank = bank_of(i, L, "hs2", b)
                    nc.vector.tensor_tensor(O[:, b, 0:H], bank[:, 0:H], HS[:, b, :], ALU.add)
                    nc.vector.tensor_tensor(O[:, b, H:3 * S], bank[:, 2 * S:H], HS[:, b, 2 * S:H], ALU.add)\
                        .then_inc(v_done, 1)
                ff(i, L, 4)
                for b in range(G):
                    low_out(i, 0, b)
                ff(i, L, 5)
                for b in range(G):
                    residual(i, 0, b)
                for b in range(G):
                    norm(i, 0, b)
                ff(i, L, 6)
                ff(i, L, 7)
                low_blocks(i, "XT0_0", hTn, 0)
                ff(i, L, 8)
                low_blocks(i, "XT0_1", hTn, 1)
                ff(i, L, 9)
                copy_chunks(i, L, "K1T", KA, CH1, True)
                for b in range(G):
                    low_part(i, "V1", b, V1, HEADS1, D1, F1)
                stream(i, *STREAMS[1], {
                    22: [lambda: low_out(i, 1, 0)],
                    23: [lambda: low_part(i, "V2", 1, V2, HEADS1, D1, F2)],
                    24: [lambda: copy_chunk(i, L, "K2T0", 0, KB, CH1), lambda: residual(i, 1, 0)]}, {}, {
                    20: [lambda: low_part(i, "V2", 0, V2, HEADS1, D1, F2)]})
                norm(i, 1, 0)
                copy_chunk(i, L, "K2T1", 1, KB, CH1)
                copy_chunk(i, L, "K2T2", 2, KB, CH1)
                low_out(i, 1, 1)
                result(i, L, 0, G)
                residual(i, 1, 1)
                low_blocks(i, "XT1_0", hTn, 0)
                norm(i, 1, 1)
                extremes_x(i + 1)
                low_blocks(i, "XT1_1", hTn, 1)
                extremes_context(i + 1)
                result(i, L, 1, G)
                diagonal(i, L)
                factors(i, L)
                stream(i, *STREAMS[2], {
                    32: [lambda: low_out(i, 2, 0), lambda: copy_chunk(i, L, "K0T1", 1, KA, CH0)],
                    34: [lambda: residual(i, 2, 0)]}, {}, {
                    30: [lambda: copy_chunk(i, L, "K0T0", 0, KA, CH0)]})
                norm(i, 2, 0)
                low_out(i, 2, 1)
                copy_chunk(i, L, "K0T2", 2, KA, CH0)
                residual(i, 2, 1)
                low_blocks(i, "XT2_0", hT3, 0)
                norm(i, 2, 1)
                assert order.next == PER["V"]
                assert links[0] == STEP_LINKS, links[0]
            order.restart()
            low_blocks(STEPS, "XT2_1", hT3, 1, TAIL_JOBS)
            for t in range(FFT):
                ff(STEPS, TAIL_JOBS, t)
            for b in range(G):
                result(STEPS, TAIL_JOBS, b, 0)

        @block.tensor
        def _(pe):
            filled = [0]

            def mm(o, lhsT, rhs, start=True, stop=True):
                return nc.tensor.matmul(o, lhsT, rhs, start=start, stop=stop)

            def j_next(i, jobs, name, k=0):
                n = jobs.number(name, k)
                assert n == filled[0], name
                filled[0] += 1
                before = last_on_bank(jobs, n)
                if before is not None:
                    back, who, number = before
                    pe.wait_ge(v_done if who == "V" else a_done, done(i - back, number, who))
                return j_bank[n % J_BANKS]

            def j_ahead(i, jobs, name, ahead):
                n = jobs.number(name)
                assert n == filled[0] + ahead and ahead < J_BANKS
                back, who, number = last_on_bank(jobs, n)
                pe.wait_ge(v_done if who == "V" else a_done, done(i - back, number, who))
                return j_bank[n % J_BANKS]

            def transposed(bank, wn, rows_k, src, at, r):
                for k, rk in enumerate(rows_k):
                    last = mm(bank[0:r, 0:GS], w[wn][0:rk, k, at:at + r], src[0:rk, k, :], k == 0,
                              k == len(rows_k) - 1)
                return last

            def transposed16(o, wn, src, at, r):
                for x, (blk, part, rows) in enumerate(PASSES):
                    last = mm(o, w16[wn][:, part, rows, at:at + r], src[:, blk, :], x == 0, x == len(PASSES) - 1)
                return last

            def natural(bank, wn, rows_k, src, b):
                for k, rk in enumerate(rows_k):
                    last = mm(bank[:, 0:H], src[0:rk, k, b * S:(b + 1) * S], w[wn][0:rk, k, :],
                              k == 0, k == len(rows_k) - 1)
                return last

            def turn(i, name, src, b, at, rows, jobs=LOOP_JOBS):
                bank = j_next(i, jobs, name)
                for k, r in enumerate(rows):
                    last = nc.tensor.transpose(bank[0:r, k * S:(k + 1) * S], src[:, b, at[k]:at[k] + r], ident[:, :])
                last.then_inc(j_full, 1)

            def v_job_done(i, jobs, name, k=0):
                pe.wait_ge(v_done, done(i, jobs.number(name, k, "V"), "V"))

            def queries_ca(i, jobs):
                for c, r in enumerate(CH0):
                    mm(j_next(i, jobs, "q1ca", c)[0:r, 0:GS], w_qca[:, AT0[c]:AT0[c] + r], caG[:, :])\
                        .then_inc(j_full, 1)

            def chunk(i, jobs, name, c, wn, rows_k, src, at, rows):
                bank = j_next(i, jobs, name, 0 if name[-1].isdigit() else c)
                transposed(bank, wn, rows_k, src, at[c], rows[c]).then_inc(j_full, 1)

            def chunks(i, jobs, name, wn, rows_k, src, at, rows):
                for c in range(3):
                    chunk(i, jobs, name, c, wn, rows_k, src, at, rows)

            def chunk16(i, name, c, wn, src):
                bank = j_next(i, LOOP_JOBS, name, 0 if name[-1].isdigit() else c)
                transposed16(bank[0:CH1[c], 0:GS], wn, src, AT1[c], CH1[c]).then_inc(j_full, 1)

            def chunks16(i, name, wn, src):
                for c in range(3):
                    chunk16(i, name, c, wn, src)

            def values(i, name, b, wn):
                natural(j_next(i, LOOP_JOBS, f"{name}_{b}"), wn, CHC, cT, b).then_inc(j_full, 1)

            def token_keys(i, jobs):
                bank = j_next(i, jobs, "kca")
                for c, r in enumerate(CH0):
                    for k, rk in enumerate(CHC):
                        last = mm(bank[0:r, c * G * T4:(c + 1) * G * T4], w["Wk_ca"][0:rk, k, AT0[c]:AT0[c] + r],
                                  cT[0:rk, k, :].rearrange("p (b s) -> p b s", b=G)[:, :, KEYS0:S], k == 0, k == 1)
                last.then_inc(j_full, 1)

            def token_values(i, jobs):
                bank = j_next(i, jobs, "vca")
                pe.wait_ge(rep_ready, i + 1)
                for k, rk in enumerate(CHC):
                    last = mm(bank[0:64, 0:H], carep[0:rk, k, :, :, :].rearrange("p b h t -> p (b h t)"),
                              w["Wv_ca"][0:rk, k, :], k == 0, k == 1)
                last.then_inc(j_full, 1)

            def stream(i, first, end, pre, mid, post, queries):
                for x in range(first, end + 3):
                    for step in pre.get(x, ()):
                        step()
                    if x < end:
                        att, b, u = ALL_UNITS[x]
                        c, h0, m = ATT_UNITS[att][u]
                        keys = KEYS[att]
                        rows = CH0 if att in (CA, FIRST) else CH1
                        Q = QB if att in (CA, SELF) else QA
                        if b == 0 and h0 == 0:
                            queries[att](c)
                        if h0 == 0:
                            pe.wait_ge(km_ready, i * CHUNKS_STEP + chunk_of(x) + 1)
                        if x >= 3:
                            pe.wait_ge(s_exp, i * UNITS_STEP + x - 2)
                        mm(s_bank[x % 3][:, 0:m * keys], Q[0:rows[c], c, b * S:(b + 1) * S],
                           KM[0:rows[c], chunk_of(x) % KM_SLOTS, h0 * keys:(h0 + m) * keys]).then_inc(s_full, 1)
                    for step in mid.get(x, ()):
                        step()
                    if first + 2 <= x < end + 2:
                        n = x - 2
                        att, _, u = ALL_UNITS[n]
                        m, keys = ATT_UNITS[att][u][2], KEYS[att]
                        bank = j_next(i, LOOP_JOBS, f"T{n}")
                        pe.wait_ge(s_exp, i * UNITS_STEP + n + 1)
                        for h in range(m):
                            last = nc.tensor.transpose(bank[0:keys, h * S:(h + 1) * S],
                                                       P[:, n % 3, h * keys:(h + 1) * keys], ident[:, :])
                        last.then_inc(j_full, 1)
                    for step in post.get(x, ()):
                        step()
                    if x >= first + 3:
                        n = x - 3
                        att, b, u = ALL_UNITS[n]
                        c, h0, m = ATT_UNITS[att][u]
                        keys = KEYS[att]
                        V, e, hc = ((VX, D0, HC0), (V0, D0, HC0), (V1, D1, HC1), (V2, D1, HC1))[att]
                        if u == 0:
                            if att == CA:
                                pe.wait_ge(vx_ready, i * G + b + 1)
                            else:
                                v_job_done(i, LOOP_JOBS, {FIRST: "V0", SELF: "V1", CROSS: "V2"}[att] + f"_{b}")
                            if att * G + b:
                                pe.wait_ge(o_done, i * (4 * G) + att * G + b)
                        v_job_done(i, LOOP_JOBS, f"T{n}")
                        for h in range(m):
                            head = sum(hc[:c]) + h0 + h
                            for y, (pp, vp) in enumerate(PV_PASSES):
                                last = mm(o_bank[:, head * (e + 1):(head + 1) * (e + 1)],
                                          PT[0:keys, n % 2, pp, h * S:(h + 1) * S], V[0:keys, b, head, vp, :],
                                          y == 0, y == len(PV_PASSES) - 1)
                        if u == len(ATT_UNITS[att]) - 1:
                            last.then_inc(o_full, 1)

            def queries_ready(i, name):
                def wait(c):
                    n = LOOP_JOBS.number(f"{name}{c}" if f"{name}{c}" in LOOP_JOBS.at else name,
                                         0 if f"{name}{c}" in LOOP_JOBS.at else c, "A")
                    pe.wait_ge(a_done, done(i, n, "A"))
                return wait

            def turn_ca(i, b):
                pe.wait_ge(o_done, i * (4 * G) + b + 1)
                turn(i, f"caT{b}", O, b, AT0, CH0)

            def turn_O(i, j, att, b):
                pe.wait_ge(o_done, i * (4 * G) + att * G + b + 1)
                turn(i, f"outT{j}_{b}", O, b, AT1, (S, S, S))

            def out_proj(i, j, b, wn):
                bank = j_next(i, LOOP_JOBS, f"outM{j}_{b}")
                v_job_done(i, LOOP_JOBS, f"outT{j}_{b}")
                for x, (blk, part, rows) in enumerate(PASSES):
                    last = mm(bank[:, 0:H], hTn[:, blk, b * S:(b + 1) * S], w16[wn][:, part, rows, :],
                              x == 0, x == len(PASSES) - 1)
                last.then_inc(j_full, 1)

            def turn_last(i, jobs):
                pe.wait_ge(xh_ready, i * (3 * G) + 1)
                turn(i, "XT2_1", XH, 1, AT1, (S, S, S), jobs)

            def turn_norm(i, j, b):
                pe.wait_ge(xh_ready, i * (3 * G) + j * G + b + 2)
                turn(i, f"XT{j}_{b}", XH, b, AT1, (S, S, S))

            def ff(i, jobs, t):
                if t == 0:
                    v_job_done(i, jobs, "XT2_1")
                bank = j_next(i, jobs, f"ff{t}")
                transposed16(bank[:, 0:GS], "ff_w1", hT3, FF + t * 128, 128)
                transposed16(bank[:, GS:2 * GS], "ff_w1", hT3, t * 128, 128).then_inc(j_full, 1)

            def ff_products(bank, b, t0, t1):
                for t in range(t0, t1):
                    last = mm(bank[:, 0:H], F[:, t, b * S:(b + 1) * S], w_ff2[:, t, :], t == 0, t == FFT - 1)
                return last

            def ff_out(i, jobs, b):
                bank = j_next(i, jobs, f"y{b}")
                if b == 0:
                    v_job_done(i, jobs, f"ff{FFT - 1}")
                ff_products(bank, b, 0, FFT).then_inc(j_full, 1)

            def extremes_turned(i, jobs):
                bank = j_next(i, jobs, "mT")
                pe.wait_ge(ext_ready, i + 2)
                nc.tensor.transpose(bank[:, 0:128], ext_wide[:, :], ident[:, :]).then_inc(j_full, 1)

            def extremes_everywhere(i, jobs):
                bank = j_next(i, jobs, "mB")
                pe.wait_ge(diag_ready, i + 2)
                mm(bank[:, 0:14], ones_square[:, :], diag[:, :]).then_inc(j_full, 1)

            def queries2_ca(i):
                v_job_done(i, LOOP_JOBS, "caT1")
                chunks(i, LOOP_JOBS, "Q2ca", "Wq", CH0, hT, AT0, CH0)

            def scores4(i):
                bank = j_next(i, LOOP_JOBS, "s4")
                queries_ready(i, "Q2ca")(2)
                for b in range(G):
                    for c, r in enumerate(CH0):
                        at = (b * HEADS0 + sum(HC0[:c])) * T4
                        last = mm(bank[:, at:at + HC0[c] * T4], QB[0:r, c, b * S:(b + 1) * S],
                                  kca[0:r, c, b, 0:HC0[c], :].rearrange("p h t -> p (h t)"))
                last.then_inc(j_full, 1)

            pe.wait_ge(stored, WAIT_BASE)
            for m, n in enumerate(("k1", "q1", "q2")):
                pe.wait_ge(raw_loaded[n], 16)
                for c, r in enumerate(CH1):
                    for k, rk in enumerate(CH1):
                        mm(j_bank[0][0:r, m * 3 + c:m * 3 + c + 1], raw[n][0:rk, k, AT1[c]:AT1[c] + r],
                           ln_b[0:rk, NORM_OF[n], k:k + 1], k == 0, k == 2)
            pe.wait_ge(raw_loaded["v1"], 16)
            for k, rk in enumerate(CH1):
                mm(j_bank[1][0:1, 0:H], ln_b[0:rk, 0, k:k + 1], raw["v1"][0:rk, k, :], k == 0, k == 2)
            pe.wait_ge(raw_loaded["ff_w1"], 16)

            def ff_shifts(t0, t1):
                for t in range(t0, t1):
                    for k, rk in enumerate(CH1):
                        last = mm(j_bank[0][:, 16 + t:17 + t], raw["ff_w1"][0:rk, k, t * 128:(t + 1) * 128],
                                  ln_b[0:rk, 2, k:k + 1], k == 0, k == 2)
                return last

            pe.wait_ge(amax_ready, 1)
            nc.tensor.transpose(j_bank[2][0:1, 0:128], amax_one_each[:, 2:3], ident[:, :]).then_inc(amax_turned, 1)
            pe.wait_ge(amax_one, 1)
            mm(j_bank[3][:, 0:1], one_row[:, :], amax_row[:, :]).then_inc(amax_all, 1)
            ff_shifts(0, 2 * FFT).then_inc(shifts_ready, 1)
            nc.tensor.transpose(j_bank[2][0:1, 0:128], amax_one_each[:, 2:3], ident[:, :])\
                .then_inc(j_full, HEAD_JOBS.skipped["J"])

            pe.wait_ge(consts_loaded, CONSTS)
            pe.wait_ge(low_ready, 1)
            pe.wait_ge(step_loaded, LOADS_STEP)
            filled[0] = HEAD_JOBS.skipped["J"]
            queries_ca(-1, HEAD_JOBS)
            chunks(-1, HEAD_JOBS, "Q0T", "Wq", CH0, xT, AT0, CH0)
            chunks(-1, HEAD_JOBS, "K0T", "Wk", CHC, cT, AT0, CH0)
            extremes_turned(-1, HEAD_JOBS)
            extremes_everywhere(-1, HEAD_JOBS)
            pe.wait_ge(a_done, PER["A"])
            pe.wait_ge(v_done, PER["V"])

            with pe.Fori(0, STEPS) as i:
                L = LOOP_JOBS
                filled[0] = 0
                stream(i, *STREAMS[0], {
                    4: [lambda: token_values(i, L)],
                    5: [lambda: turn_last(i, L)],
                    7: [lambda: turn_ca(i, 0)],
                    10: [lambda: turn_ca(i, 1)],
                    11: [lambda: queries2_ca(i)],
                    12: [lambda: scores4(i)],
                    14: [lambda: ff(i, L, 1)]}, {
                    2: [lambda: token_keys(i, L)]}, {
                    6: [lambda: values(i, "V0", 0, "Wv")],
                    9: [lambda: values(i, "V0", 1, "Wv")],
                    12: [lambda: ff(i, L, 0)]},
                    {CA: queries_ready(i - 1, "q1ca"), FIRST: queries_ready(i - 1, "Q0T")})
                ff(i, L, 2)
                pe.wait_ge(p4_ready, i + 1)
                nc.tensor.transpose(j_next(i, L, "p4T")[:, 0:128], p4_wide[:, :, :].rearrange("p q t -> p (q t)"),
                                    ident[:, :]).then_inc(j_full, 1)
                ff(i, L, 3)
                v_job_done(i, L, "p4T")
                for b in range(G):
                    rows = slice(b * HEADS0 * T4, (b + 1) * HEADS0 * T4)
                    mm(j_next(i, L, "hs2", b)[:, 0:H], p4T[rows, :], vca[rows, :]).then_inc(j_full, 1)
                ff(i, L, 4)
                for b in range(G):
                    v_job_done(i, L, "hs2", b)
                    turn(i, f"outT0_{b}", O, b, AT1, (S, S, S))
                ff(i, L, 5)
                for b in range(G):
                    out_proj(i, 0, b, "Wout")
                ff(i, L, 6)
                ff(i, L, 7)
                turn_norm(i, 0, 0)
                ff(i, L, 8)
                turn_norm(i, 0, 1)
                ff(i, L, 9)
                v_job_done(i, L, "XT0_1")
                chunks16(i, "K1T", "k1", hTn)
                for b in range(G):
                    bank = j_next(i, L, f"V1_{b}")
                    for x, (blk, part, rows) in enumerate(PASSES):
                        mm(bank[:, 0:H], hTn[:, blk, b * S:(b + 1) * S], w16["v1"][:, part, rows, :], x == 0, False)
                    mm(bank[:, 0:H], one_row[:, :], v_b[:, :], False, True).then_inc(j_full, 1)
                chunks16(i, "Q1T", "q1", hTn)
                stream(i, *STREAMS[1], {
                    22: [lambda: turn_O(i, 1, SELF, 0)],
                    23: [lambda: values(i, "V2", 1, "v2")],
                    24: [lambda: chunk(i, L, "K2T0", 0, "k2", CHC, cT, AT1, CH1), lambda: out_proj(i, 1, 0, "o1_w")]}, {}, {
                    20: [lambda: values(i, "V2", 0, "v2")]},
                    {SELF: queries_ready(i, "Q1T")})
                chunk(i, L, "K2T1", 1, "k2", CHC, cT, AT1, CH1)
                chunk(i, L, "K2T2", 2, "k2", CHC, cT, AT1, CH1)
                turn_O(i, 1, SELF, 1)
                ff_out(i, L, 0)
                out_proj(i, 1, 1, "o1_w")
                turn_norm(i, 1, 0)
                bank = j_ahead(i, L, "y1", 1)
                ff_products(bank, 1, 0, 7)
                turn_norm(i, 1, 1)
                j_next(i, L, "y1")
                ff_products(bank, 1, 7, FFT).then_inc(j_full, 1)
                v_job_done(i, L, "XT1_1")
                chunk16(i, "Q2T0", 0, "q2", hTn)
                extremes_turned(i, L)
                chunk16(i, "Q2T1", 1, "q2", hTn)
                extremes_everywhere(i, L)
                chunk16(i, "Q2T2", 2, "q2", hTn)
                stream(i, *STREAMS[2], {
                    32: [lambda: turn_O(i, 2, CROSS, 0),
                         lambda: chunk(i, L, "K0T1", 1, "Wk", CHC, cT, AT0, CH0)],
                    33: [lambda: chunk(i, L, "Q0T0", 0, "Wq", CH0, xT, AT0, CH0)],
                    34: [lambda: out_proj(i, 2, 0, "o2_w")]}, {}, {
                    30: [lambda: pe.wait_ge(step_loaded, i * LOADS_STEP + 2 * LOADS_STEP),
                         lambda: chunk(i, L, "K0T0", 0, "Wk", CHC, cT, AT0, CH0)]},
                    {CROSS: queries_ready(i, "Q2T")})
                queries_ca(i, L)
                chunk(i, L, "Q0T1", 1, "Wq", CH0, xT, AT0, CH0)
                turn_O(i, 2, CROSS, 1)
                chunk(i, L, "K0T2", 2, "Wk", CHC, cT, AT0, CH0)
                out_proj(i, 2, 1, "o2_w")
                turn_norm(i, 2, 0)
                chunk(i, L, "Q0T2", 2, "Wq", CH0, xT, AT0, CH0)
                assert filled[0] == PER["J"]
            filled[0] = 0
            turn_last(STEPS, TAIL_JOBS)
            for t in range(FFT):
                ff(STEPS, TAIL_JOBS, t)
            for b in range(G):
                ff_out(STEPS, TAIL_JOBS, b)


def kernel(**inputs):
    import numpy as np
    import concourse.bacc as bacc
    from concourse.bass_utils import run_bass_kernel_spmd

    p = {n.split("_xattn_")[-1]: np.ascontiguousarray(a) for n, a in inputs.items()}
    x, c = (np.concatenate([a, a[:1]]) for a in
            (p["x"].reshape(STEPS, G, S, H), p["ctx_768"].reshape(STEPS, G, S, C)))
    arrays = {
        "x": x,
        "xT": x.transpose(0, 3, 1, 2).reshape(STEPS + 1, H, GS),
        "cT": c.transpose(0, 3, 1, 2).reshape(STEPS + 1, C, GS),
    }
    channels = np.linspace(0, C - 1, S).astype(np.int64)
    arrays["caG"] = c[:, :, KEYS0:, :][:, :, :, channels].transpose(0, 2, 1, 3).reshape(STEPS + 1, T4, GS)
    for n in MATS0 + MATSC + ("ff_w2", "Wq_ca"):
        arrays[n] = p[n]
    for n in MATSN:
        arrays[n] = np.concatenate([p[n], p[n][AT1[2]:]])

    def chunked(v):
        out = np.zeros((128, 3), v.dtype)
        for k, r in enumerate(CH1):
            out[:r, k] = v[AT1[k]:AT1[k] + r]
        out[64:, 2] = v[AT1[2]:]
        return out

    arrays["bias"] = np.broadcast_to(np.stack([p[n] for n in ("b_out", "o1_b", "o2_b", "ff_b2")]), (128, 4, H))
    arrays["ln_g"] = np.stack([chunked(p[f"n{j}_g"]) for j in (1, 2, 3)] + [np.ones((128, 3), np.float32)], 1)
    arrays["ln_b"] = np.stack([chunked(p[f"n{j}_b"]) for j in (1, 2, 3)], 1)
    arrays["ff_b"] = p["ff_b1"].reshape(2 * FFT, 128).T
    arrays["ident"] = np.eye(128, dtype=np.float32)
    arrays["mask0"] = (np.arange(120)[:, None] // D0 == np.arange(3)).astype(np.float32) * np.float32(D0 ** -0.5)
    arrays["mask1"] = (np.arange(128)[:, None] // D1 == np.arange(8)).astype(np.float32) * np.float32(D1 ** -0.5)
    arrays["maskv"] = (np.arange(64)[:, None] // T4 % HEADS0 == np.arange(H) // D0).astype(np.float32)

    nc = bacc.Bacc("TRN2", target_bir_lowering=False, num_devices=1)
    arrays = {n: np.ascontiguousarray(a) for n, a in arrays.items()}
    d = {n: nc.dram_tensor(f"in_{n}", a.shape, mybir.dt.from_np(a.dtype), kind="ExternalInput").ap()
         for n, a in arrays.items()}
    out = nc.dram_tensor("out_0", (STEPS, G, S, H), mybir.dt.float32, kind="ExternalOutput").ap()
    build(nc, d, out)
    r = run_bass_kernel_spmd(nc, [{f"in_{n}": a for n, a in arrays.items()}], core_ids=[0])
    return r.results[0]["out_0"].reshape(B, S, H)
```
